# Optimizing a Trainium2 kernel written in Bass

```python
import numpy as np
import jax
import jax.numpy as jnp

def _softmax(x, axis=-1):
    return jax.nn.softmax(x, axis=axis)

def _gelu(x):
    return jax.nn.gelu(x, approximate=True)

def _silu(x):
    return jax.nn.silu(x)

def _sigmoid(x):
    return jax.nn.sigmoid(x)

def _layernorm(x, axis=-1, eps=1e-05):
    m = jnp.mean(x, axis=axis, keepdims=True)
    v = jnp.var(x, axis=axis, keepdims=True)
    return (x - m) / jnp.sqrt(v + eps)

def _scatter_add(tgt, idx, src, axis=0):
    return tgt.at[idx].add(src)

def _segment_sum(src, seg, n):
    return jax.ops.segment_sum(src, seg, n)
kernel_name = 'mk_prb_d1_jaxref_r8_6d6c79'

def setup_inputs(seed: int=0):
    np.random.seed(seed)
    _w = jnp.asarray

    def _L0_attn_setup():
        import jax, jax.numpy as jnp
        import numpy as np
        EMBED = 128
        DSTATE = 16
        DCONV = 4
        DTRANK = 64
        B = 2
        T = 256
        key = jax.random.key(seed)
        ks = jax.random.split(key, 8)

        def w(k, shape, s=0.02):
            return jax.random.normal(k, shape, dtype=jnp.float32) * s
        return dict(x=jax.random.normal(ks[0], (B, T, EMBED), dtype=jnp.float32), in_proj_w=w(ks[1], (2 * EMBED, EMBED)), in_proj_b=jnp.zeros((2 * EMBED,), jnp.float32), conv_w=w(ks[2], (EMBED, 1, DCONV)), conv_b=jnp.zeros((EMBED,), jnp.float32), x_proj_w=w(ks[3], (DTRANK + 2 * DSTATE, EMBED)), x_proj_b=jnp.zeros((DTRANK + 2 * DSTATE,), jnp.float32), dt_proj_w=w(ks[4], (EMBED, DTRANK)), dt_proj_b=jnp.zeros((EMBED,), jnp.float32), A_log=jnp.log(jnp.arange(1, DSTATE + 1, dtype=jnp.float32))[None, :], D_param=jnp.ones((EMBED,), jnp.float32), out_proj_w=w(ks[5], (EMBED, EMBED)), out_proj_b=jnp.zeros((EMBED,), jnp.float32), skip_proj_w=w(ks[6], (EMBED, EMBED)), skip_proj_b=jnp.zeros((EMBED,), jnp.float32))
    _L0_attn_in = _L0_attn_setup()

    def _L0_ffn_setup():
        import jax, jax.numpy as jnp
        import numpy as np
        B, T, D, F, E = (2, 128, 128, 512, 8)
        EPS = 1e-06
        key = jax.random.key(seed)
        k = jax.random.split(key, 5)
        scale = 0.02
        return {'x': jax.random.normal(k[0], (B, T, D), dtype=jnp.float32), 'rms_w': jnp.ones((D,), dtype=jnp.float32), 'gate_w': jax.random.normal(k[1], (E, D), dtype=jnp.float32) * scale, 'W1': jax.random.normal(k[2], (E, D, F), dtype=jnp.float32) * scale, 'b1': jnp.zeros((E, F), dtype=jnp.float32), 'W2': jax.random.normal(k[3], (E, F, D), dtype=jnp.float32) * scale, 'b2': jnp.zeros((E, D), dtype=jnp.float32)}
    _L0_ffn_in = _L0_ffn_setup()
    _d = {'L0_attn_x': _L0_attn_in['x'], 'L0_attn_in_proj_w': _L0_attn_in['in_proj_w'], 'L0_attn_in_proj_b': _L0_attn_in['in_proj_b'], 'L0_attn_conv_w': _L0_attn_in['conv_w'], 'L0_attn_conv_b': _L0_attn_in['conv_b'], 'L0_attn_x_proj_w': _L0_attn_in['x_proj_w'], 'L0_attn_x_proj_b': _L0_attn_in['x_proj_b'], 'L0_attn_dt_proj_w': _L0_attn_in['dt_proj_w'], 'L0_attn_dt_proj_b': _L0_attn_in['dt_proj_b'], 'L0_attn_A_log': _L0_attn_in['A_log'], 'L0_attn_D_param': _L0_attn_in['D_param'], 'L0_attn_out_proj_w': _L0_attn_in['out_proj_w'], 'L0_attn_out_proj_b': _L0_attn_in['out_proj_b'], 'L0_attn_skip_proj_w': _L0_attn_in['skip_proj_w'], 'L0_attn_skip_proj_b': _L0_attn_in['skip_proj_b'], 'L0_ffn_rms_w': _L0_ffn_in['rms_w'], 'L0_ffn_gate_w': _L0_ffn_in['gate_w'], 'L0_ffn_W1': _L0_ffn_in['W1'], 'L0_ffn_b1': _L0_ffn_in['b1'], 'L0_ffn_W2': _L0_ffn_in['W2'], 'L0_ffn_b2': _L0_ffn_in['b2']}
    _x0 = _d['L0_attn_x']
    _d['L0_attn_x'] = jax.random.normal(jax.random.fold_in(jax.random.key(seed), 1), (4, 1024, 128), dtype=_x0.dtype)
    del _x0
    return _d

def reference(L0_attn_x, L0_attn_in_proj_w, L0_attn_in_proj_b, L0_attn_conv_w, L0_attn_conv_b, L0_attn_x_proj_w, L0_attn_x_proj_b, L0_attn_dt_proj_w, L0_attn_dt_proj_b, L0_attn_A_log, L0_attn_D_param, L0_attn_out_proj_w, L0_attn_out_proj_b, L0_attn_skip_proj_w, L0_attn_skip_proj_b, L0_ffn_rms_w, L0_ffn_gate_w, L0_ffn_W1, L0_ffn_b1, L0_ffn_W2, L0_ffn_b2):

    def _L0_attn_ref(x, in_proj_w, in_proj_b, conv_w, conv_b, x_proj_w, x_proj_b, dt_proj_w, dt_proj_b, A_log, D_param, out_proj_w, out_proj_b, skip_proj_w, skip_proj_b):
        import jax, jax.numpy as jnp
        import numpy as np
        EMBED = 128
        DSTATE = 16
        DCONV = 4
        DTRANK = 64
        B = 2
        T = 256
        Bsz, Tlen, Dm = x.shape
        xr = x @ in_proj_w.T + in_proj_b
        x_in, res = jnp.split(xr, 2, axis=-1)
        xc = jax.lax.conv_general_dilated(x_in.transpose(0, 2, 1), conv_w, (1,), [(DCONV - 1, 0)], dimension_numbers=('NCH', 'OIH', 'NCH'), feature_group_count=Dm)
        xc = (xc + conv_b[None, :, None]).transpose(0, 2, 1)
        xc = jax.nn.silu(xc)
        ssm = xc @ x_proj_w.T + x_proj_b
        delta, Bp, Cp = jnp.split(ssm, [DTRANK, DTRANK + DSTATE], axis=-1)
        delta = jax.nn.softplus(delta @ dt_proj_w.T + dt_proj_b)
        A = -jnp.exp(A_log)
        dA = jnp.exp(delta[..., None] * A)
        dBu = delta[..., None] * Bp[:, :, None, :] * xc[..., None]

        def op(l, r):
            Ai, Bi = l
            Aj, Bj = r
            return (Aj * Ai, Bj + Aj * Bi)
        _, ys = jax.lax.associative_scan(op, (dA, dBu), axis=1)
        y = (ys * Cp[:, :, None, :]).sum(-1)
        y = y + xc * D_param
        y = y * jax.nn.silu(res)
        return y @ out_proj_w.T + out_proj_b + (x @ skip_proj_w.T + skip_proj_b)

    def _L0_ffn_ref(x, rms_w, gate_w, W1, b1, W2, b2):
        import jax, jax.numpy as jnp
        import numpy as np
        B, T, D, F, E = (2, 128, 128, 512, 8)
        EPS = 1e-06
        ms = jnp.mean(x * x, axis=-1, keepdims=True)
        xn = x * jax.lax.rsqrt(ms + EPS) * rms_w
        logits = jnp.einsum('btd,ed->bte', xn, gate_w)
        scores = jax.nn.softmax(logits, axis=-1)
        top1_idx = jnp.argmax(scores, axis=-1)
        top1_score = jnp.max(scores, axis=-1)
        out = jnp.zeros_like(xn)
        for e in range(E):
            h = jax.nn.silu(jnp.einsum('btd,df->btf', xn, W1[e]) + b1[e])
            ye = jnp.einsum('btf,fd->btd', h, W2[e]) + b2[e]
            out = jnp.where((top1_idx == e)[..., None], ye, out)
        return out * top1_score[..., None]
    x = L0_attn_x
    xn = _layernorm(x, axis=-1)
    x = x + _L0_attn_ref(xn, L0_attn_in_proj_w, L0_attn_in_proj_b, L0_attn_conv_w, L0_attn_conv_b, L0_attn_x_proj_w, L0_attn_x_proj_b, L0_attn_dt_proj_w, L0_attn_dt_proj_b, L0_attn_A_log, L0_attn_D_param, L0_attn_out_proj_w, L0_attn_out_proj_b, L0_attn_skip_proj_w, L0_attn_skip_proj_b) + _L0_ffn_ref(xn, L0_ffn_rms_w, L0_ffn_gate_w, L0_ffn_W1, L0_ffn_b1, L0_ffn_W2, L0_ffn_b2)
    return x

_drawn_inputs = setup_inputs


def setup_inputs(seed=0):
    import zlib

    import numpy as np

    out = dict(_drawn_inputs(seed))
    spreads = {'L0_attn_in_proj_b': (0.0, 0.8),
     'L0_attn_conv_b': (0.0, 0.8),
     'L0_attn_x_proj_b': (0.0, 0.8),
     'L0_attn_dt_proj_b': (0.0, 0.8),
     'L0_attn_D_param': (1.0, 0.6),
     'L0_attn_out_proj_b': (0.0, 0.8),
     'L0_attn_skip_proj_b': (0.0, 0.8),
     'L0_ffn_rms_w': (1.0, 0.6),
     'L0_ffn_b1': (0.0, 2.0),
     'L0_ffn_b2': (0.0, 2.0)}
    factors = {'L0_attn_in_proj_w': 8.0,
     'L0_attn_conv_w': 8.0,
     'L0_attn_x_proj_w': 8.0,
     'L0_attn_dt_proj_w': 8.0,
     'L0_attn_A_log': 8.0,
     'L0_attn_out_proj_w': 8.0,
     'L0_ffn_gate_w': 3.093,
     'L0_ffn_W1': 6.078,
     'L0_ffn_W2': 5.604,
     'L0_attn_skip_proj_w': 5.654}
    for name, (base, spread) in spreads.items():
        noise = np.random.default_rng([zlib.crc32(name.encode()), seed]).standard_normal(out[name].shape)
        drawn = base * np.exp(spread * noise) if base else spread * noise
        out[name] = jnp.asarray(drawn.astype(out[name].dtype))
    for name, factor in factors.items():
        out[name] = (out[name] * factor).astype(out[name].dtype)
    return out
```

```python
from contextlib import ExitStack

import concourse.bass as bass
from concourse import mybir

F32 = mybir.dt.float32
BF16 = mybir.dt.bfloat16
I32 = mybir.dt.int32
ALU = mybir.AluOpType
ACT = mybir.ActivationFunctionType
AX_X = mybir.AxisListType.X

P = 128
B, T, D = 4, 1024, 128
N = 16
K = 4
R = 64
E, F = 8, 512
L = 512
HALVES = T // L
CH = B * HALVES
BPC = L // P
NB = CH * BPC
EC = P // N
UNITS = D // EC
UB = UNITS * HALVES
QUADS = 4
FC = F // P
TILES = NB + E - 1
TPB = TILES // (B - 1)
assert TPB * (B - 1) == TILES
LN_EPS, RMS_EPS = 1e-5, 1e-6
SOFTPLUS_CUT = 30.0
RING_B, RING_P = 4, 8
GAT = 4
AHEAD = 2

DVE_P = {15, 31, 14, 30}
DVE_P_LAST = {15, 31, 14, 30, 1, 3, 5, 7, 9, 11, 13, 17, 19, 21, 23, 25, 27, 29}

def slot_turn(i): return 2 * i + 2
def slot_hidden(i): return 2 * i + 3
def slot_gate(i): return 2 * i + 4
def slot_down(i): return 2 * i + 5


def before(units, w):
    return sum(1 for x in units if x < w)


def block_program(nc, x, w_in, w_x, w_dt, w_out, w_skip, w_gate, w_exp, b1b2, cols, out_b2,
                  ident_in, strict_in, sel_in, red_in, first_in, tile_in, out):
    pool_units = [w for w in range(UB) if w not in DVE_P]
    pool_last = [w for w in range(UB) if w not in DVE_P_LAST]
    NP, ND = len(pool_units), len(DVE_P)

    with ExitStack() as ctx:
        def sb(name, shape, dt=F32):
            return ctx.enter_context(nc.sbuf_tensor(name, shape, dt))

        def sem(name):
            return ctx.enter_context(nc.semaphore(name))

        acc = sb("acc", [P, NB, D])
        dd = sb("dd", [P, CH, 2, L])
        xc = sb("xc", [P, CH, L])
        sres = sb("sres", [P, CH, L])
        hst = sb("hst", [P, UNITS, L])
        xr = hst[:, UNITS // 2:UNITS, :].rearrange("p u (j d) -> p (u j) d", d=D)
        dbu = sb("dbu", [P, RING_B, L])
        ch_ = sb("ch", [P, RING_P, L])
        brep = sb("brep", [P, HALVES, L])
        crep = sb("crep", [P, HALVES, L])
        parts = sb("parts", [P, 3, 2 * L], BF16)
        rest = sb("rest", [P, 2 * L])
        stack = sb("stack", [P, HALVES, 2, 4, L], BF16)
        y1 = sb("y1", [P, L])
        yg = sb("yg", [P, L])
        wst = sb("wst", [P, 2, 2 * F])
        bst = sb("bst", [3, 2, F + D], BF16)
        xs = sb("xs", [P, 2, D])
        xsT = sb("xsT", [P, P])
        th = sb("th", [P, F])
        hid = sb("hid", [P, F])
        ysb = sb("ysb", [P, 2, D])
        xin = [dbu[:, 0:2, :].rearrange("p a l -> p (a l)")[:, 0:L + K - 1],
               dbu[:, 2:4, :].rearrange("p a l -> p (a l)")[:, 0:L + K - 1]]
        conv = [ch_[:, i, :] for i in range(2)]
        low = [ch_[0:R, 2 + i, :] for i in range(2)]
        soft_z = [ch_[:, 4 + i, :] for i in range(2)]
        soft_l = [ch_[:, 6 + i, :] for i in range(2)]
        xn = [hst[:, i, :].rearrange("p (j d) -> p j d", d=D) for i in range(2)]
        gat = sb("gat", [P, GAT, D])

        ident = sb("ident", [P, P])
        strict = sb("strict", [P, P])
        ones = sb("ones", [P, P])
        sel = sb("sel", [P, P], BF16)
        red = sb("red", [P, 4, 32])
        win = sb("win", [P, 2 * D])
        wx = sb("wx", [P, R + 2 * P])
        wdt = sb("wdt", [R, D])
        wout = sb("wout", [P, D])
        wskip = sb("wskip", [P, D])
        wgate = sb("wgate", [P, E])
        col = sb("col", [P, 10 + K])
        lowb, rms, cw = col[0:R, 8:9], col[:, 9:10], col[:, 10:10 + K]
        ob = sb("ob", [2, D])
        nega = sb("nega", [P, 2])
        onesb = sb("onesb", [3, P], BF16)
        bb = wst[0:E, :, :].rearrange("p s f -> p (s f)")[:, 0:3 * (F + D)].rearrange("p (k f) -> p k f", k=3)
        bbp = crep[0:E, :, :].bitcast(BF16).rearrange("p h t -> p (h t)")[:, 0:3 * (F + D)].rearrange("p (k f) -> p k f", k=3)

        stats = sb("stats", [P, NB, 6])
        mv = sb("mv", [P, NB, 2])
        sm = sb("sm", [P, 12, NB])
        rt = hst[:, 2:5, :].rearrange("p u l -> p (u l)").rearrange("p (k e j) -> p k e j", k=6, e=E)
        first = sb("first", [P, E, NB])
        cnt = sb("cnt", [P, 6, E])
        cnti = sb("cnti", [P, E], I32)
        posi = sb("posi", [P, NB], I32)
        tilec = sb("tilec", [1, TILES, E])
        tcmp = sb("tcmp", [1, TILES, E])
        tef = sb("tef", [1, TILES])
        tei = sb("tei", [1, TILES], I32)
        score = sb("score", [P, NB])
        zero = th

        bank = [ctx.enter_context(nc.psum_tensor(f"bank{i}", [P, 512], F32)) for i in range(8)]
        bank_d, bank_u, bank_y, bank_h, bank_m, bank_f = bank[0:2], bank[2:4], bank[4], bank[5], bank[6], bank[7]

        rows_in = nc.dram_tensor("rows_in", [TILES * P, D], F32, kind="Internal").ap()
        rows_out = nc.dram_tensor("rows_out", [TILES * P, D], F32, kind="Internal").ap()
        bias_parts = nc.dram_tensor("bias_parts", [E, 3, F + D], BF16, kind="Internal").ap()
        part_rows = nc.dram_tensor("part_rows", [D, 3, 2, L], BF16, kind="Internal").ap()

        x_in = [sem(f"x_in{c}") for c in range(CH)]
        consts_in = sem("consts_in")
        gate_in = sem("gate_in")
        rows_zeroed = sem("rows_zeroed")
        bias_stored = sem("bias_stored")
        scattered = sem("scattered")
        tile_in_s = [sem(f"tile_in{i}") for i in range(2)]
        ys_stored = [sem(f"ys_stored{i}") for i in range(2)]
        gathered = [sem(f"gathered{i}") for i in range(GAT)]
        parts_stored = sem("parts_stored")
        stack_in = sem("stack_in")
        out_stored = sem("out_stored")
        const_made = sem("const_made")
        zero_made = sem("zero_made")
        sel_made = sem("sel_made")
        expa_made = sem("expa_made")
        nega_made = sem("nega_made")
        gatew_made = sem("gatew_made")
        aggregated = sem("aggregated")
        score_made = sem("score_made")
        stat_made = sem("stat_made")
        small = sem("small")
        ln_made = sem("ln_made")
        rs_ready = sem("rs_ready")
        xn_made = sem("xn_made")
        xr_made = sem("xr_made")
        xt_turned = sem("xt_turned")
        xt_copied = sem("xt_copied")
        skip_made = sem("skip_made")
        gate_made = sem("gate_made")
        skip_added = sem("skip_added")
        inx_made = sem("inx_made")
        inres_made = sem("inres_made")
        xin_copied = sem("xin_copied")
        tap_made = sem("tap_made")
        conv_step = sem("conv_step")
        pad_made = sem("pad_made")
        xc_made = sem("xc_made")
        sres_made = sem("sres_made")
        low_made = sem("low_made")
        low_copied = sem("low_copied")
        dt_made = sem("dt_made")
        z_made = sem("z_made")
        e_made = sem("e_made")
        l_made = sem("l_made")
        delta_made = sem("delta_made")
        du_made = sem("du_made")
        route = sem("route")
        rexp_made = sem("rexp_made")
        rank_made = sem("rank_made")
        routed = sem("routed")
        bsplit = sem("bsplit")
        repd = sem("repd")
        repu = sem("repu")
        exped = sem("exped")
        mulb = sem("mulb")
        scanned = sem("scanned")
        pool_p = sem("pool_p")
        dve_p = sem("dve_p")
        reduced = sem("reduced")
        y1_made = sem("y1_made")
        yg_made = sem("yg_made")
        proj_made = sem("proj_made")
        acc_added = sem("acc_added")
        hi_made = sem("hi_made")
        rest_made = sem("rest_made")
        mid_made = sem("mid_made")
        lo_made = sem("lo_made")
        brep_mm = sem("brep_mm")
        brep_ready = sem("brep_ready")
        crep_mm = sem("crep_mm")
        crep_ready = sem("crep_ready")
        xs_turned = sem("xs_turned")
        xs_copied = sem("xs_copied")
        hidden = sem("hidden")
        tanh_made = sem("tanh_made")
        gated = sem("gated")
        down = sem("down")
        ys_copied = sem("ys_copied")
        combined = sem("combined")

        CONSTS = [(win, w_in), (wx, w_x), (wdt, w_dt), (wout, w_out), (wskip, w_skip), (col, cols),
                  (ob, out_b2), (strict, strict_in), (sel, None),
                  (red, red_in), (first, first_in), (tilec, tile_in)]
        x_blocks = x.rearrange("b (n p) d -> p (b n) d", p=P)
        out_blocks = out.rearrange("b (n p) d -> p (b n) d", p=P)

        BANKS, GROUPS, SLOTS = 2, 2, 2
        CREDITS = [(scanned, BANKS), (mulb, BANKS), (reduced, GROUPS), (down, SLOTS), (gated, 1), (acc_added, 1),
                   (y1_made, 1), (ys_copied, 1), (pool_p, NP), (dve_p, ND), (ys_stored[0], 16), (ys_stored[1], 16)]

        def dd_of(c):
            if isinstance(c, int):
                return dd[:, c, :, :].rearrange("p w t -> p (w t)")
            return dd[:, bass.ds(c, 1), :, :].rearrange("p a w t -> p (a w t)")

        def row_of(tile, c):
            if isinstance(c, int):
                return tile[:, c, :]
            return tile[:, bass.ds(c, 1), :].rearrange("p a t -> p (a t)")

        def blocks_of(c):
            if isinstance(c, int):
                return acc[:, BPC * c:BPC * c + BPC, :]
            return acc[:, bass.ds(c * BPC, BPC), :]

        block = ctx.enter_context(nc.Block())

        @block.sync
        def _(sp):
            for credited, n in CREDITS:
                sp.sem_inc(credited, n)
            for c in range(CH):
                sp.dma_start(acc[:, BPC * c:BPC * c + BPC, :], x_blocks[:, BPC * c:BPC * c + BPC, :]).then_inc(x_in[c], 16)
                if c == 1:
                    sp.dma_start(ident[:, :], ident_in).then_inc(gate_in, 16)
                    sp.dma_start(wgate[:, :], w_gate).then_inc(gate_in, 16)
                    sp.dma_start(bb[:, 0, :], b1b2).then_inc(gate_in, 16)
            for dst, src in CONSTS:
                if src is None:
                    sp.dma_start(rest[:, 0:P], sel_in).then_inc(consts_in, 16)
                    continue
                sp.dma_start(dst[tuple(slice(None) for _ in dst.shape)], src).then_inc(consts_in, 16)
            sp.wait_ge(zero_made, 1)
            sp.dma_start(rows_in[0:TILES // 3 * P, :].rearrange("(n p) d -> p n d", p=P),
                         zero[:, 0:P].unsqueeze(1).broadcast_to([P, TILES // 3, P])).then_inc(rows_zeroed, 16)
            sp.dma_start(rows_in[TILES // 3 * P:2 * TILES // 3 * P, :].rearrange("(n p) d -> p n d", p=P),
                         zero[:, 0:P].unsqueeze(1).broadcast_to([P, TILES // 3, P])).then_inc(rows_zeroed, 16)
            sp.dma_start(rows_in[2 * TILES // 3 * P:, :].rearrange("(n p) d -> p n d", p=P),
                         zero[:, 0:P].unsqueeze(1).broadcast_to([P, TILES // 3, P])).then_inc(rows_zeroed, 16)
            sp.wait_ge(bsplit, 6)
            sp.dma_start(bias_parts, bbp[:, :, :]).then_inc(bias_stored, 16)

            def load_stack(c, h):
                sp.wait_ge(lo_made, c + 1)
                if not (isinstance(c, int) and c == 0):
                    sp.wait_ge(repd, UNITS * (c - 1) + 1)
                    sp.wait_ge(repu, UNITS * (c - 1) + 1)
                sp.dma_start(part_rows.rearrange("d k w t -> d (k w t)"),
                             parts[:, :, :].rearrange("p k t -> p (k t)")).then_inc(parts_stored, 16)
                sp.wait_ge(parts_stored, 16 * (c + 1))
                for q in range(QUADS):
                    for w in range(2):
                        src = part_rows[32 * q:32 * q + 32].rearrange("(m e) k w t -> (e k) w m t", m=4)
                        sp.dma_start(stack[32 * q:32 * q + 3 * EC, h, w, :, :], src[:, w, :, :]).then_inc(stack_in, 16)

            load_stack(0, 0)
            sp.wait_ge(bias_stored, 16)
            sp.wait_ge(scattered, 16 * NB)
            sp.wait_ge(routed, 2)

            def load_tile(b, i):
                t = b * TPB + i
                s = i % 2
                sp.wait_ge(down, t + (1 if i else 2))
                e = sp.value_load(tei[0:1, bass.ds(t, 1)], min_val=0, max_val=E - 1)
                sp.dma_start(wst[:, s, :], w_exp[bass.ds(e, 1)].rearrange("a p f -> p (a f)")).then_inc(tile_in_s[s], 16)
                sp.dma_start(bst[:, s, :], bias_parts[bass.ds(e, 1)].rearrange("a k f -> k (a f)")).then_inc(tile_in_s[s], 16)
                sp.dma_start(xs[:, s, :], rows_in[bass.ds(t * P, P), :]).then_inc(tile_in_s[s], 16)

            def batch(b, last):
                for w in range(UB):
                    h, u = divmod(w, UNITS)
                    if u == 13 and not (last and h == HALVES - 1):
                        load_stack(b * HALVES + h + 1, (h + 1) % 2)
                    if not last:
                        for i in range(TPB):
                            if w == max(0, slot_down(i - 2) if i > 1 else 0):
                                load_tile(b, i)

            with sp.Fori(0, B - 1) as b:
                batch(b, False)
            batch(B - 1, True)
            for c in range(CH):
                sp.wait_ge(combined, BPC * (c + 1))
                sp.dma_start(out_blocks[:, BPC * c:BPC * c + BPC, :], acc[:, BPC * c:BPC * c + BPC, :]).then_inc(out_stored, 16)
            sp.wait_ge(out_stored, 16 * CH)

        @block.gpsimd
        def _(pool):
            pool.memset(zero[:, :], 0.0).then_inc(zero_made, 1)
            pool.memset(ones[:, :], 1.0).then_inc(const_made, 1)
            pool.memset(onesb[:, :], 1.0).then_inc(const_made, 1)
            for c in range(CH):
                pool.wait_ge(small, 12)
                pool.wait_ge(xn_made, BPC * (c + 1))
                pool.tensor_tensor(xr[:, BPC * c:BPC * c + BPC, :], xn[c % 2],
                                   sm[:, 9, BPC * c:BPC * c + BPC].unsqueeze(2).broadcast_to([P, BPC, D]),
                                   ALU.mult).then_inc(xr_made, 1)
            pool.wait_ge(xr_made, CH)
            pool.wait_ge(rows_zeroed, 48)
            pool.wait_ge(routed, 1)
            for j in range(NB):
                pool.indirect_dma_start(out=rows_in[:, :], out_offset=bass.IndirectOffsetOnAxis(ap=posi[:, j:j + 1], axis=0),
                                        in_=xr[:, j, :], in_offset=None).then_inc(scattered, 16)

            def split_rest(c):
                pool.wait_ge(hi_made, c + 1)
                pool.tensor_tensor(rest[:, :], dd_of(c), parts[:, 0, :], ALU.subtract).then_inc(rest_made, 1)

            def split_lo(c):
                pool.wait_ge(mid_made, c + 1)
                pool.tensor_tensor(parts[:, 2, :], rest[:, :], parts[:, 1, :], ALU.subtract).then_inc(lo_made, 1)

            pool.wait_ge(sel_made, 1)
            split_rest(0)
            split_lo(0)

            def batch(b, last):
                units = pool_last if last else pool_units
                for w in range(UB):
                    h, u = divmod(w, UNITS)
                    c = b * HALVES + h
                    more = not (last and h == HALVES - 1)
                    if u == 3 and more:
                        split_rest(c + 1)
                    if u == 8 and more:
                        split_lo(c + 1)
                    if w in units:
                        pool.wait_ge(scanned, b * UB + w + 1 + 2)
                        pool.wait_ge(crep_ready, c + 1)
                        pool.wait_ge(reduced, 4 * c + u // 4 - 1 + 2)
                        pool.tensor_tensor(ch_[:, u % RING_P, :], hst[:, u, :], crep[:, h, :], ALU.mult).then_inc(pool_p, 1)
                    if last:
                        j = w
                        if j == 0:
                            for s in range(2):
                                pool.wait_ge(ys_stored[s], 16 * (((TPB + 1 - s) // 2) * (B - 1) + 1))
                        if j >= GAT:
                            pool.wait_ge(combined, j - GAT + 1)
                        pool.indirect_dma_start(out=gat[:, j % GAT, :], out_offset=None, in_=rows_out[:, :],
                                                in_offset=bass.IndirectOffsetOnAxis(ap=posi[:, j:j + 1], axis=0)
                                                ).then_inc(gathered[j % GAT], 16)

            with pool.Fori(0, B - 1) as b:
                batch(b, False)
            batch(B - 1, True)

        @block.scalar
        def _(act):
            def rsqrt_guess(n, src, lg, guess):
                act.wait_ge(small, n)
                act.activation(lg, src, ACT.Ln).then_inc(ln_made, 1)
                act.wait_ge(ln_made, 1 if n == 1 else 3)
                act.activation(guess, lg, ACT.Exp, scale=-0.5).then_inc(ln_made, 1)

            rsqrt_guess(1, sm[:, 0, :], sm[:, 1, :], sm[:, 2, :])
            rsqrt_guess(8, sm[:, 5, :], sm[:, 6, :], sm[:, 7, :])
            act.wait_ge(consts_in, 16 * len(CONSTS))
            act.activation(nega[:, 0:1], col[:, 5:6], ACT.Exp).then_inc(expa_made, 1)
            act.activation(sel[:, :], rest[:, 0:P], ACT.Copy).then_inc(sel_made, 1)
            for c in range(CH):
                act.wait_ge(xt_turned, c + 1)
                act.activation(dd[:, c, 1, :], bank[c % 2][:, :], ACT.Copy).then_inc(xt_copied, 1)
                act.wait_ge(inx_made, c + 1)
                if c >= 2:
                    act.wait_ge(conv_step, 3 * (c - 1))
                    act.wait_ge(pad_made, 1 + c // 2)
                act.activation(xin[c % 2][:, K - 1:], bank[5][:, :], ACT.Identity, bias=col[:, 0:1]).then_inc(xin_copied, 1)
                act.wait_ge(xin_copied, c + 1)
                if c >= 2:
                    act.wait_ge(xc_made, c - 1)
                act.activation(conv[c % 2], xin[c % 2][:, K - 1:], ACT.Identity, bias=col[:, 2:3],
                               scale=cw[:, K - 1:K]).then_inc(tap_made, 1)
                act.wait_ge(inres_made, c + 1)
                act.activation(sres[:, c, :], bank[6][:, :], ACT.Silu, bias=col[:, 1:2]).then_inc(sres_made, 1)
                if c >= 1:
                    act.wait_ge(conv_step, 3 * c)
                    act.activation(xc[:, c - 1, :], conv[(c - 1) % 2], ACT.Silu).then_inc(xc_made, 1)
            act.wait_ge(conv_step, 3 * CH)
            act.activation(xc[:, CH - 1, :], conv[(CH - 1) % 2], ACT.Silu).then_inc(xc_made, 1)
            act.wait_ge(route, 3)
            act.activation(rt[:, 1], rt[:, 0], ACT.Exp).then_inc(rexp_made, 1)

            def soft(c):
                act.wait_ge(z_made, c + 1)
                act.activation(soft_z[c % 2], soft_z[c % 2], ACT.Exp).then_inc(e_made, 1)
                act.wait_ge(e_made, c + 1)
                if c >= 2:
                    act.wait_ge(delta_made, c - 1)
                act.activation(soft_l[c % 2], soft_z[c % 2], ACT.Ln, bias=1.0).then_inc(l_made, 1)

            for c in range(CH):
                act.wait_ge(low_made, c + 1)
                if c >= 2:
                    act.wait_ge(dt_made, c - 1)
                act.activation(low[c % 2], bank[7][0:R, :], ACT.Identity, bias=lowb).then_inc(low_copied, 1)
                if c >= 1:
                    soft(c - 1)
            soft(CH - 1)

            def split_hi(c):
                act.wait_ge(du_made, CH)
                if not (isinstance(c, int) and c == 0):
                    act.wait_ge(parts_stored, 16 * c)
                act.activation(parts[:, 0, :], dd_of(c), ACT.Copy).then_inc(hi_made, 1)

            def split_mid(c):
                act.wait_ge(rest_made, c + 1)
                act.activation(parts[:, 1, :], rest[:, :], ACT.Copy).then_inc(mid_made, 1)

            def brep_copy(c, h):
                act.wait_ge(brep_mm, c + 1)
                if not (isinstance(c, int) and c == 0):
                    act.wait_ge(mulb, UNITS * (c - 1) + 1 + BANKS)
                act.activation(brep[:, h, :], bank_f[:, :], ACT.Identity, bias=col[:, 6:7]).then_inc(brep_ready, 1)

            def crep_copy(c, h):
                act.wait_ge(crep_mm, c + 1)
                if not (isinstance(c, int) and c == 0):
                    act.wait_ge(reduced, 4 * (c - 1) + GROUPS)
                act.activation(crep[:, h, :], bank_f[:, :], ACT.Identity, bias=col[:, 7:8]).then_inc(crep_ready, 1)

            def decay(b, w):
                act.wait_ge(repd, b * UB + w + 1)
                act.activation(bank_d[w % 2][:, :], bank_d[w % 2][:, :], ACT.Exp, scale=nega[:, 1:2]).then_inc(exped, 1)

            act.wait_ge(nega_made, 1)
            split_hi(0)
            brep_copy(0, 0)
            act.wait_ge(bias_stored, 16)
            crep_copy(0, 0)
            split_mid(0)
            decay(0, 0)
            decay(0, 1)

            def batch(b, last):
                for w in range(UB):
                    h, u = divmod(w, UNITS)
                    c = b * HALVES + h
                    more = not (last and h == HALVES - 1)
                    hn = (h + 1) % 2
                    if more and u == 2:
                        split_hi(c + 1)
                    if more and u == 7:
                        split_mid(c + 1)
                    if more and u == 4:
                        brep_copy(c + 1, hn)
                    if more and u == 9:
                        crep_copy(c + 1, hn)
                    if not last:
                        for i in range(TPB):
                            t = b * TPB + i
                            if w == slot_turn(i):
                                act.wait_ge(xs_turned, t + 1)
                                act.activation(xsT[:, :], bank_m[:, 0:P], ACT.Copy, scale=rms).then_inc(xs_copied, 1)
                            if w == slot_hidden(i):
                                act.wait_ge(hidden, t + 1)
                                act.wait_ge(gated, t + 1)
                                act.activation(th[:, :], bank_h[:, :], ACT.Tanh, scale=0.5).then_inc(tanh_made, 1)
                            if w == slot_down(i):
                                s = i % 2
                                act.wait_ge(down, t + 1 + 2)
                                act.wait_ge(ys_stored[s], 16 * (b * ((TPB + 1 - s) // 2) + i // 2 + 1))
                                act.activation(ysb[:, s, :], bank_m[:, P:2 * P], ACT.Copy).then_inc(ys_copied, 1)
                                act.wait_ge(ys_copied, t + 1 + 1)
                                act.dma_start(rows_out[bass.ds(t * P, P), :], ysb[:, s, :]).then_inc(ys_stored[s], 16)
                    if not (last and w + AHEAD >= UB):
                        decay(b, w + AHEAD) if w + AHEAD < UB else decay(b + 1, w + AHEAD - UB)

            with act.Fori(0, B - 1) as b:
                batch(b, False)
            batch(B - 1, True)


        @block.vector
        def _(dve):
            steps = [0]

            def stat(ins):
                steps[0] += 1
                ins.then_inc(small, 1)
                dve.wait_ge(small, steps[0])

            dve.memset(xin[0][:, 0:K - 1], 0.0).then_inc(pad_made, 1)
            for j in range(NB):
                if j % BPC == 0:
                    dve.wait_ge(x_in[j // BPC], 16)
                dve.bn_stats(stats[:, j, :], acc[:, j, :]).then_inc(stat_made, 1)
            dve.wait_ge(stat_made, NB)
            for j in range(NB):
                dve.bn_aggr(mv[:, j, :], stats[:, j, :]).then_inc(aggregated, 1)
            dve.wait_ge(aggregated, NB)
            var = mv[:, :, 1]
            stat(dve.tensor_scalar(sm[:, 0, :], var, LN_EPS, None, ALU.add))

            def newton(value, guess, tmp, result):
                stat(dve.tensor_tensor(tmp, guess, guess, ALU.mult))
                stat(dve.tensor_tensor(tmp, tmp, value, ALU.mult))
                stat(dve.tensor_scalar(tmp, tmp, -0.5, 1.5, ALU.mult, ALU.add))
                stat(dve.tensor_tensor(result, guess, tmp, ALU.mult))

            dve.wait_ge(ln_made, 2)
            newton(sm[:, 0, :], sm[:, 2, :], sm[:, 3, :], sm[:, 4, :])
            stat(dve.tensor_tensor(sm[:, 8, :], var, sm[:, 4, :], ALU.mult))
            stat(dve.tensor_tensor(sm[:, 8, :], sm[:, 8, :], sm[:, 4, :], ALU.mult))
            stat(dve.tensor_scalar(sm[:, 5, :], sm[:, 8, :], RMS_EPS, None, ALU.add))

            def normalise(c):
                if c >= 2:
                    dve.wait_ge(xt_turned, c - 1)
                    dve.wait_ge(xr_made, c - 1)
                for j in range(BPC):
                    n = BPC * c + j
                    dve.tensor_scalar(xn[c % 2][:, j, :], acc[:, n, :], mv[:, n, 0:1], sm[:, 4, n:n + 1],
                                      ALU.subtract, ALU.mult).then_inc(xn_made, 1)

            normalise(0)
            dve.wait_ge(ln_made, 4)
            newton(sm[:, 5, :], sm[:, 7, :], sm[:, 3, :], sm[:, 9, :])
            normalise(1)
            dve.wait_ge(gate_in, 48)
            dve.wait_ge(consts_in, 16 * len(CONSTS))
            dve.tensor_scalar(wgate[:, :], wgate[:, :], rms, None, ALU.mult).then_inc(gatew_made, 1)
            made = [0]

            def bias(ins):
                made[0] += 1
                ins.then_inc(bsplit, 1)
                dve.wait_ge(bsplit, made[0])

            bias(dve.tensor_scalar(bb[:, 0, F:], bb[:, 0, F:], 2.0, None, ALU.mult))
            bias(dve.tensor_copy(bbp[:, 0, :], bb[:, 0, :]))
            bias(dve.tensor_tensor(bb[:, 1, :], bb[:, 0, :], bbp[:, 0, :], ALU.subtract))
            bias(dve.tensor_copy(bbp[:, 1, :], bb[:, 1, :]))
            bias(dve.tensor_tensor(bb[:, 2, :], bb[:, 1, :], bbp[:, 1, :], ALU.subtract))
            bias(dve.tensor_copy(bbp[:, 2, :], bb[:, 2, :]))
            dve.wait_ge(expa_made, 1)
            dve.tensor_scalar(nega[:, 1:2], nega[:, 0:1], -1.0, None, ALU.mult).then_inc(nega_made, 1)

            def convolve(c):
                if c % 2:
                    dve.wait_ge(xin_copied, c)
                    dve.tensor_copy(xin[1][:, 0:K - 1], xin[0][:, L:L + K - 1]).then_inc(pad_made, 1)
                    dve.wait_ge(pad_made, 2 + c // 2)
                dve.wait_ge(tap_made, c + 1)
                for n, k in enumerate(range(K - 2, -1, -1)):
                    if n:
                        dve.wait_ge(conv_step, 3 * c + n)
                    dve.scalar_tensor_tensor(out=conv[c % 2], in0=xin[c % 2][:, k:k + L], scalar=cw[:, k:k + 1],
                                             in1=conv[c % 2], op0=ALU.mult, op1=ALU.add).then_inc(conv_step, 1)

            for c in range(CH):
                dve.wait_ge(skip_made, c + 1)
                dve.tensor_tensor(acc[:, BPC * c:BPC * c + BPC, :], acc[:, BPC * c:BPC * c + BPC, :],
                                  bank[2 + c % 2][:, :].rearrange("p (j d) -> p j d", d=D), ALU.add).then_inc(skip_added, 1)
                if c + 2 < CH:
                    normalise(c + 2)
                convolve(c)

            done = [0]

            def step(ins):
                done[0] += 1
                ins.then_inc(route, 1)
                dve.wait_ge(route, done[0])

            def per_token(v):
                return v.unsqueeze(1).broadcast_to([P, E, NB])

            def by_token(v):
                return v.rearrange("p e j -> p j e")

            dve.wait_ge(gate_made, CH)
            step(dve.tensor_tensor(rt[:, 0], bank[4][:, 0:NB * E].rearrange("p (j e) -> p e j", e=E), per_token(sm[:, 9, :]), ALU.mult))
            step(dve.tensor_reduce(sm[:, 10, :], by_token(rt[:, 0]), AX_X, ALU.max))
            step(dve.tensor_tensor(rt[:, 0], rt[:, 0], per_token(sm[:, 10, :]), ALU.subtract))
            dve.wait_ge(rexp_made, 1)
            step(dve.tensor_reduce(sm[:, 11, :], by_token(rt[:, 1]), AX_X, ALU.add))
            step(dve.reciprocal(score[:, :], sm[:, 11, :]))
            step(dve.tensor_scalar(score[:, :], score[:, :], 0.5, None, ALU.mult))
            step(dve.scalar_tensor_tensor(out=rt[:, 2], in0=rt[:, 0], scalar=0.0, in1=first[:, :, :],
                                          op0=ALU.is_equal, op1=ALU.mult))
            step(dve.tensor_reduce(sm[:, 10, :], by_token(rt[:, 2]), AX_X, ALU.max))
            step(dve.tensor_tensor(rt[:, 3], rt[:, 2], per_token(sm[:, 10, :]), ALU.is_equal))
            one_hot = done[0]
            assert one_hot == 9
            dve.wait_ge(rank_made, 1)
            within = bank[2][:, 0:E * NB].rearrange("p (e j) -> p e j", e=E)
            total = bank[2][:, E * NB:2 * E * NB].rearrange("p (e j) -> p e j", e=E)
            for e in range(E):
                step(dve.tensor_tensor_scan(rt[:, 4, e, :], ones[:, 0:NB], total[:, e, :], 0.0, ALU.mult, ALU.add))
            step(dve.tensor_scalar(cnti[:, :], rt[:, 4, :, NB - 1], float(P - 1), None, ALU.add))
            step(dve.tensor_scalar(cnti[:, :], cnti[:, :], 7, 7, ALU.logical_shift_right, ALU.logical_shift_left))
            step(dve.tensor_copy(cnt[:, 1, :], cnti[:, :]))
            step(dve.tensor_tensor_scan(cnt[:, 2, :], ones[:, 0:E], cnt[:, 1, :], 0.0, ALU.mult, ALU.add))
            step(dve.tensor_tensor(cnt[:, 3, :], cnt[:, 2, :], cnt[:, 1, :], ALU.subtract))
            step(dve.tensor_tensor(rt[:, 5], within, rt[:, 4], ALU.add))
            step(dve.tensor_tensor(rt[:, 5], rt[:, 5], total, ALU.subtract))
            step(dve.tensor_tensor(rt[:, 5], rt[:, 5], cnt[:, 3, :].unsqueeze(2).broadcast_to([P, E, NB]), ALU.add))
            step(dve.tensor_tensor(rt[:, 5], rt[:, 5], rt[:, 3], ALU.mult))
            step(dve.tensor_reduce(sm[:, 10, :], by_token(rt[:, 5]), AX_X, ALU.add))
            dve.tensor_copy(posi[:, :], sm[:, 10, :]).then_inc(routed, 1)
            step(dve.tensor_tensor(tcmp[:, :, :], tilec[:, :, :], cnt[0:1, 2, :].unsqueeze(1).broadcast_to([1, TILES, E]), ALU.is_ge))
            step(dve.tensor_reduce(tef[:, :], tcmp[:, :, :], AX_X, ALU.add))
            dve.tensor_scalar(tei[:, :], tef[:, :], float(E - 1), None, ALU.min).then_inc(routed, 1)

            def cut(c):
                dve.wait_ge(dt_made, c + 1)
                if c >= 2:
                    dve.wait_ge(l_made, c - 1)
                dve.tensor_scalar(soft_z[c % 2], bank[c % 2][:, :], col[:, 3:4], SOFTPLUS_CUT, ALU.add, ALU.min).then_inc(z_made, 1)

            cut(0)
            for c in range(CH):
                if c + 1 < CH:
                    cut(c + 1)
                dve.wait_ge(l_made, c + 1)
                dve.scalar_tensor_tensor(out=dd[:, c, 0, :], in0=bank[c % 2][:, :], scalar=col[:, 3:4], in1=soft_l[c % 2],
                                         op0=ALU.add, op1=ALU.max).then_inc(delta_made, 1)
                if c >= 1:
                    dve.wait_ge(delta_made, c)
                    dve.tensor_tensor(dd[:, c - 1, 1, :], dd[:, c - 1, 0, :], xc[:, c - 1, :], ALU.mult).then_inc(du_made, 1)
            dve.wait_ge(delta_made, CH)
            dve.tensor_tensor(dd[:, CH - 1, 1, :], dd[:, CH - 1, 0, :], xc[:, CH - 1, :], ALU.mult).then_inc(du_made, 1)

            def drive(b, w):
                h, u = divmod(w, UNITS)
                dve.wait_ge(repu, b * UB + w + 1)
                dve.wait_ge(brep_ready, b * HALVES + h + 1)
                dve.tensor_tensor(dbu[:, w % RING_B, :], bank_u[w % 2][:, :], brep[:, h, :], ALU.mult).then_inc(mulb, 1)

            def scan(b, w, last):
                h, u = divmod(w, UNITS)
                dve.wait_ge(exped, b * UB + w + 1)
                dve.wait_ge(mulb, b * UB + w + 1 + BANKS)
                v, units_p, units_d = (w - UNITS, pool_last, DVE_P_LAST) if last and w >= UNITS else (w - UNITS, pool_units, DVE_P)
                back = 0 if v >= 0 else 1
                v %= UB
                if v in units_d:
                    dve.wait_ge(dve_p, (b - back) * ND + before(units_d, v) + 1 + ND)
                else:
                    dve.wait_ge(pool_p, (b - back) * NP + before(units_p, v) + 1 + NP)
                if w == UNITS // 2:
                    dve.wait_ge(scattered, 16 * NB)
                start = hst[:, u, L - 1:L] if h else 0.0
                dve.tensor_tensor_scan(hst[:, u, :], bank_d[w % 2][:, :], dbu[:, w % RING_B, :], start,
                                       ALU.mult, ALU.add).then_inc(scanned, 1)

            drive(0, 0)
            drive(0, 1)

            def combine(j):
                dve.wait_ge(gathered[j % GAT], 16 * (j // GAT + 1))
                dve.scalar_tensor_tensor(out=acc[:, j, :], in0=gat[:, j % GAT, :], scalar=score[:, j:j + 1],
                                         in1=acc[:, j, :], op0=ALU.mult, op1=ALU.add).then_inc(combined, 1)

            def batch(b, last):
                for w in range(UB):
                    h, u = divmod(w, UNITS)
                    c = b * HALVES + h
                    scan(b, w, last)
                    if w + AHEAD < UB:
                        drive(b, w + AHEAD)
                    elif not last:
                        drive(b + 1, w + AHEAD - UB)
                    if not last:
                        for i in range(TPB):
                            if w == slot_gate(i):
                                t = b * TPB + i
                                dve.wait_ge(tanh_made, t + 1)
                                dve.wait_ge(down, t + SLOTS)
                                dve.scalar_tensor_tensor(out=hid[:, :], in0=th[:, :], scalar=1.0, in1=bank_h[:, :],
                                                         op0=ALU.add, op1=ALU.mult).then_inc(gated, 1)
                    elif w >= 2 and w - 2 < NB - BPC:
                        combine(w - 2)
                    if w in (DVE_P_LAST if last else DVE_P):
                        dve.wait_ge(scanned, b * UB + w + 1 + BANKS)
                        dve.wait_ge(crep_ready, c + 1)
                        dve.wait_ge(reduced, 4 * c + u // 4 - 1 + GROUPS)
                        dve.tensor_tensor(ch_[:, u % RING_P, :], hst[:, u, :], crep[:, h, :], ALU.mult).then_inc(dve_p, 1)
                    if u == UNITS - 1:
                        dve.wait_ge(reduced, 4 * (c + 1) + GROUPS)
                        dve.scalar_tensor_tensor(out=y1[:, :], in0=row_of(xc, c), scalar=col[:, 4:5], in1=bank_y[:, :],
                                                 op0=ALU.mult, op1=ALU.add).then_inc(y1_made, 1)
                        dve.wait_ge(y1_made, c + 1 + 1)
                        dve.tensor_tensor(yg[:, :], y1[:, :], row_of(sres, c), ALU.mult).then_inc(yg_made, 1)
                        dve.wait_ge(proj_made, c + 1)
                        dve.tensor_tensor(blocks_of(c), blocks_of(c), bank_f[:, :].rearrange("p (j d) -> p j d", d=D),
                                          ALU.add).then_inc(acc_added, 1)
                if last:
                    dve.wait_ge(acc_added, CH + 1)
                    for j in range(NB - BPC if UB - 2 >= NB - BPC else UB - 2, NB):
                        combine(j)

            with dve.Fori(0, B - 1) as b:
                batch(b, False)
            batch(B - 1, True)

        @block.tensor
        def _(pe):
            def turn(c):
                pe.wait_ge(xn_made, BPC * (c + 1))
                if c >= 2:
                    pe.wait_ge(xt_copied, c - 1)
                for j in range(BPC):
                    mm = pe.transpose(bank[c % 2][:, P * j:P * j + P], xn[c % 2][:, j, :], ident[:, :])
                mm.then_inc(xt_turned, 1)

            pe.wait_ge(gate_in, 48)
            turn(0)
            for c in range(CH):
                if c + 1 < CH:
                    turn(c + 1)
                if c == 0:
                    pe.wait_ge(consts_in, 16 * len(CONSTS))
                    pe.wait_ge(const_made, 2)
                    pe.wait_ge(gatew_made, 1)
                pe.wait_ge(xt_copied, c + 1)
                xt = dd[:, c, 1, :]
                if c >= 1:
                    pe.wait_ge(xin_copied, c)
                pe.matmul(bank[5][:, :], win[:, 0:D], xt, start=True, stop=True).then_inc(inx_made, 1)
                if c >= 1:
                    pe.wait_ge(sres_made, c)
                pe.matmul(bank[6][:, :], win[:, D:2 * D], xt, start=True, stop=True).then_inc(inres_made, 1)
                if c >= 2:
                    pe.wait_ge(skip_added, c - 1)
                for j in range(BPC):
                    o = bank[2 + c % 2][:, P * j:P * j + P]
                    pe.matmul(o, ones[0:2, :], ob[:, :], start=True, stop=False)
                    mm = pe.matmul(o, xt[:, P * j:P * j + P], wskip[:, :], start=False, stop=True)
                mm.then_inc(skip_made, 1)
                for j in range(BPC):
                    n = BPC * c + j
                    mm = pe.matmul(bank[4][:, E * n:E * n + E], xt[:, P * j:P * j + P], wgate[:, :], start=True, stop=True)
                mm.then_inc(gate_made, 1)
            pe.wait_ge(route, 9)
            pe.wait_ge(skip_added, CH)
            pe.matmul(bank[2][:, 0:E * NB], strict[:, :], rt[:, 3].rearrange("p e j -> p (e j)"), start=True, stop=True)
            pe.matmul(bank[2][:, E * NB:2 * E * NB], ones[:, :], rt[:, 3].rearrange("p e j -> p (e j)"),
                      start=True, stop=True).then_inc(rank_made, 1)

            def low_rank(c):
                pe.wait_ge(xc_made, c + 1)
                if c >= 1:
                    pe.wait_ge(low_copied, c)
                pe.matmul(bank[7][0:R, :], wx[:, 0:R], xc[:, c, :], start=True, stop=True).then_inc(low_made, 1)

            low_rank(0)
            for c in range(CH):
                if c + 1 < CH:
                    low_rank(c + 1)
                pe.wait_ge(low_copied, c + 1)
                if c >= 2:
                    pe.wait_ge(delta_made, c - 1)
                pe.matmul(bank[c % 2][:, :], wdt[:, :], low[c % 2], start=True, stop=True).then_inc(dt_made, 1)

            def brep_matmul(c):
                if isinstance(c, int) and c == 0:
                    pe.wait_ge(low_copied, CH)
                else:
                    pe.wait_ge(acc_added, c - 1 + 1)
                pe.matmul(bank_f[:, :], wx[:, R:R + P], row_of(xc, c), start=True, stop=True).then_inc(brep_mm, 1)

            def crep_matmul(c):
                pe.wait_ge(brep_ready, c + 1)
                pe.matmul(bank_f[:, :], wx[:, R + P:R + 2 * P], row_of(xc, c), start=True, stop=True).then_inc(crep_mm, 1)

            def rep_u(b, w):
                h, u = divmod(w, UNITS)
                m, q = divmod(u, QUADS)
                if u == 0:
                    pe.wait_ge(stack_in, 16 * 2 * QUADS * (b * HALVES + h + 1))
                pe.wait_ge(mulb, b * UB + w - 1 + BANKS)
                rows = slice(32 * q, 32 * q + 3 * EC)
                pe.matmul(bank_u[w % 2][:, :], sel[rows, :], stack[rows, h, 1, m, :], start=True, stop=True,
                          tile_position=(32 * q, 0)).then_inc(repu, 1)

            def rep_d(b, w):
                h, u = divmod(w, UNITS)
                m, q = divmod(u, QUADS)
                pe.wait_ge(scanned, b * UB + w - 1 + BANKS)
                rows = slice(32 * q, 32 * q + 3 * EC)
                pe.matmul(bank_d[w % 2][:, :], sel[rows, :], stack[rows, h, 0, m, :], start=True, stop=True,
                          tile_position=(32 * q, 0)).then_inc(repd, 1)

            brep_matmul(0)
            crep_matmul(0)
            pe.wait_ge(du_made, CH)
            pe.wait_ge(routed, 2)
            pe.wait_ge(sel_made, 1)
            for w in range(AHEAD):
                rep_u(0, w)
                rep_d(0, w)

            def reduce(b, h, m, last):
                c = b * HALVES + h
                end = h * UNITS + 4 * m + 4
                units_p, units_d = (pool_last, DVE_P_LAST) if last else (pool_units, DVE_P)
                pe.wait_ge(pool_p, b * NP + before(units_p, end) + NP)
                pe.wait_ge(dve_p, b * ND + before(units_d, end) + ND)
                if m == 0:
                    pe.wait_ge(y1_made, c + 1)
                for q in range(QUADS):
                    mm = pe.matmul(bank_y[32 * q:32 * q + 32, :], red[:, m, :], ch_[:, (4 * m + q) % RING_P, :],
                                   start=(m == 0), stop=(m == 3), tile_position=(0, 32 * q))
                mm.then_inc(reduced, 1)

            def batch(b, last):
                for w in range(UB):
                    h, u = divmod(w, UNITS)
                    c = b * HALVES + h
                    more = not (last and h == HALVES - 1)
                    nxt = (b, w + AHEAD) if w + AHEAD < UB else (b + 1, w + AHEAD - UB)
                    if not (last and w + AHEAD >= UB):
                        rep_u(*nxt)
                    if more and u == 3:
                        brep_matmul(c + 1)
                    if more and u == 8:
                        crep_matmul(c + 1)
                    if u in (6, 10, 14):
                        reduce(b, h, u // 4 - 1 if u != 14 else 2, last)
                    if not last:
                        for i in range(TPB):
                            t, s = b * TPB + i, i % 2
                            if w == slot_down(i):
                                pe.wait_ge(gated, t + 1 + 1)
                                pe.wait_ge(ys_copied, t + 1)
                                if i + 1 < TPB:
                                    pe.wait_ge(xs_copied, t + 2)
                                pe.matmul(bank_m[:, P:2 * P], onesb[:, :], bst[:, s, F:F + D], start=True, stop=False)
                                for f in range(FC):
                                    mm = pe.matmul(bank_m[:, P:2 * P], hid[:, P * f:P * f + P],
                                                   wst[:, s, F + D * f:F + D * f + D], start=False, stop=(f == FC - 1))
                                mm.then_inc(down, 1)
                            if w == slot_turn(i):
                                pe.wait_ge(tile_in_s[s], 48 * (b * ((TPB + 1 - s) // 2) + i // 2 + 1))
                                pe.wait_ge(ys_copied, t if i else t + 1)
                                pe.transpose(bank_m[:, 0:P], xs[:, s, :], ident[:, :]).then_inc(xs_turned, 1)
                            if w == slot_hidden(i):
                                pe.wait_ge(xs_copied, t + 1)
                                pe.wait_ge(gated, t + 1)
                                for f in range(FC):
                                    o = bank_h[:, P * f:P * f + P]
                                    pe.matmul(o, bst[:, s, P * f:P * f + P], onesb[:, :], start=True, stop=False)
                                    mm = pe.matmul(o, wst[:, s, P * f:P * f + P], xsT[:, :], start=False, stop=True)
                                mm.then_inc(hidden, 1)
                    if not (last and w + AHEAD >= UB):
                        rep_d(*nxt)
                    if u == UNITS - 1:
                        reduce(b, h, 3, last)
                        pe.wait_ge(yg_made, c + 1)
                        pe.wait_ge(crep_ready, (c + 2) if more else CH)
                        for j in range(BPC):
                            mm = pe.matmul(bank_f[:, P * j:P * j + P], yg[:, P * j:P * j + P], wout[:, :], start=True, stop=True)
                        mm.then_inc(proj_made, 1)

            with pe.Fori(0, B - 1) as b:
                batch(b, False)
            batch(B - 1, True)


def kernel(**inputs):
    import numpy as np
    import concourse.bacc as bacc
    from concourse.bass_utils import run_bass_kernel_spmd as run

    a = {k: np.asarray(v) for k, v in inputs.items()}
    at = lambda n: a["L0_attn_" + n]
    ff = lambda n: a["L0_ffn_" + n]
    xp = at("x_proj_w").T
    xb = at("x_proj_b")
    cols = np.stack([at("in_proj_b")[:D], at("in_proj_b")[D:], at("conv_b"), at("dt_proj_b"), at("D_param"),
                     np.repeat(at("A_log")[0], EC), np.repeat(xb[R:R + N], EC), np.repeat(xb[R + N:], EC),
                     np.concatenate([xb[:R], xb[:R]]), ff("rms_w")] + [at("conv_w")[:, 0, k] for k in range(K)], axis=1)
    w1 = ff("W1")
    w2 = ff("W2").reshape(E, FC, P, D).transpose(0, 2, 1, 3).reshape(E, P, FC * D)
    n = np.arange(P)
    sel = np.zeros((P, P), np.float32)
    for q in range(QUADS):
        for e in range(EC):
            for k in range(3):
                sel[32 * q + 3 * e + k, e::EC] = 1.0
    red = np.zeros((P, 4, 32), np.float32)
    for m in range(4):
        red[n, m, EC * m + n % EC] = 1.0
    arrays = {
        "x": at("x"), "w_in": at("in_proj_w").T,
        "w_x": np.concatenate([xp[:, :R], np.repeat(xp[:, R:R + N], EC, axis=1), np.repeat(xp[:, R + N:], EC, axis=1)], axis=1),
        "w_dt": at("dt_proj_w").T, "w_out": at("out_proj_w").T, "w_skip": at("skip_proj_w").T, "w_gate": ff("gate_w").T,
        "w_exp": np.concatenate([w1, w2], axis=2), "b1b2": np.concatenate([ff("b1"), ff("b2")], axis=1),
        "cols": cols,
        "out_b2": np.stack([at("out_proj_b"), at("skip_proj_b")]),
        "ident": np.eye(P, dtype=np.float32), "strict": np.triu(np.ones((P, P), np.float32), 1), "sel": sel, "red": red,
        "first": np.ascontiguousarray(np.broadcast_to((E - np.arange(E, dtype=np.float32))[None, :, None], (P, E, NB))),
        "tiles": np.ascontiguousarray(np.broadcast_to((P * np.arange(TILES, dtype=np.float32))[None, :, None], (1, TILES, E))),
    }
    nc = bacc.Bacc("TRN2", target_bir_lowering=False, num_devices=1)
    arrays = {f"in_{k}_dram": np.ascontiguousarray(v) for k, v in arrays.items()}
    args = [nc.dram_tensor(k, v.shape, mybir.dt.from_np(v.dtype), kind="ExternalInput").ap() for k, v in arrays.items()]
    args.append(nc.dram_tensor("out_0_dram", (B, T, D), F32, kind="ExternalOutput").ap())
    block_program(nc, *args)
    r = run(nc, [arrays], core_ids=[0])
    return r.results[0]["out_0_dram"]
```

```python
from contextlib import ExitStack

import concourse.bass as bass
from concourse import mybir

F32 = mybir.dt.float32
BF16 = mybir.dt.bfloat16
I32 = mybir.dt.int32
ALU = mybir.AluOpType
ACT = mybir.ActivationFunctionType
AX_X = mybir.AxisListType.X

P = 128
B, T, D = 4, 1024, 128
N = 16
K = 4
R = 64
E, F = 8, 512
L = 512
HALVES = T // L
CH = B * HALVES
BPC = L // P
NB = CH * BPC
EC = P // N
UNITS = D // EC
UB = UNITS * HALVES
QUADS = 4
FC = F // P
TILES = NB + E - 1
TPB = TILES // (B - 1)
assert TPB * (B - 1) == TILES
LN_EPS, RMS_EPS = 1e-5, 1e-6
SOFTPLUS_CUT = 30.0
RING_B, RING_P = 4, 8
GAT = 4
AHEAD = 2
HEAD = 4
assert HEAD <= UNITS

DVE_P = {15, 31, 14, 30}
DVE_P_LAST = {15, 31, 14, 30, 5, 7, 9, 11, 13, 17, 19, 21, 23, 25, 27, 29}
assert all(w >= HEAD for w in DVE_P | DVE_P_LAST)


def slot_turn(i): return 2 * i + 2 if i else HEAD
def slot_hidden(i): return 2 * i + 4
def slot_gate(i): return 2 * i + 5
def slot_down(i): return 2 * i + 7


SLOT_HI, SLOT_REST, SLOT_MID, SLOT_LO, SLOT_STORE, SLOT_STACK, SLOT_B, SLOT_C = 0, 1, 3, 4, 6, 8, 5, 9


def batches(engine, slot):
    for w in range(HEAD):
        slot(0, w, True, False)
    with engine.Fori(0, B - 1) as b:
        for w in range(HEAD, UB):
            slot(b, w, False, False)
        for w in range(HEAD):
            slot(b + 1, w, False, False)
    for w in range(HEAD, UB):
        slot(B - 1, w, False, True)


def gathers(w):
    if w < HEAD:
        return []
    return [2 * (w - HEAD), 2 * (w - HEAD) + 1] if w < 2 * HEAD else [w]


def before(units, w):
    return sum(1 for x in units if x < w)


def block_program(nc, x, w_in, w_x, w_dt, w_out, w_skip, w_gate, w_exp, b1b2, cols, out_b2,
                  ident_in, strict_in, sel_in, red_in, first_in, tile_in, out):
    pool_units = [w for w in range(UB) if w not in DVE_P]
    pool_last = [w for w in range(UB) if w not in DVE_P_LAST]
    NP, ND = len(pool_units), len(DVE_P)

    with ExitStack() as ctx:
        def sb(name, shape, dt=F32):
            return ctx.enter_context(nc.sbuf_tensor(name, shape, dt))

        def sem(name):
            return ctx.enter_context(nc.semaphore(name))

        acc = sb("acc", [P, NB, D])
        dd = sb("dd", [P, CH, 2, L])
        xc = sb("xc", [P, CH, L])
        sres = sb("sres", [P, CH, L])
        hst = sb("hst", [P, UNITS, L])
        xr = hst[:, UNITS // 2:UNITS, :].rearrange("p u (j d) -> p (u j) d", d=D)
        dbu = sb("dbu", [P, RING_B, L])
        ch_ = sb("ch", [P, RING_P, L])
        brep = sb("brep", [P, HALVES, L])
        crep = sb("crep", [P, HALVES, L])
        parts = sb("parts", [P, 3, 2 * L], BF16)
        rest = sb("rest", [P, 2 * L])
        stack = sb("stack", [P, HALVES, 4, 2, L], BF16)
        y1 = sb("y1", [P, L])
        yg = sb("yg", [P, L])
        wst = sb("wst", [P, 2, 2 * F])
        bst = sb("bst", [3, 2, F + D], BF16)
        xs = sb("xs", [P, 2, D])
        xsT = sb("xsT", [P, P])
        th = sb("th", [P, F])
        hid = sb("hid", [P, 2, F])
        ysb = sb("ysb", [P, 2, D])
        xin = [dbu[:, 0:2, :].rearrange("p a l -> p (a l)")[:, 0:L + K - 1],
               dbu[:, 2:4, :].rearrange("p a l -> p (a l)")[:, 0:L + K - 1]]
        conv = [ch_[:, i, :] for i in range(2)]
        low = [ch_[0:R, 2 + i, :] for i in range(2)]
        soft_z = [ch_[:, 4 + i, :] for i in range(2)]
        soft_l = [ch_[:, 6 + i, :] for i in range(2)]
        xn = [hst[:, i, :].rearrange("p (j d) -> p j d", d=D) for i in range(2)]
        gat = sb("gat", [P, GAT, D])

        ident = sb("ident", [P, P])
        strict = sb("strict", [P, P])
        ones = sb("ones", [P, P])
        sel = sb("sel", [P, P], BF16)
        red = sb("red", [P, 4, 32])
        win = sb("win", [P, 2 * D])
        wx = sb("wx", [P, R + 2 * P])
        wdt = sb("wdt", [R, D])
        wout = sb("wout", [P, D])
        wskip = sb("wskip", [P, D])
        wgate = sb("wgate", [P, E])
        col = sb("col", [P, 10 + K])
        lowb, rms, cw = col[0:R, 8:9], col[:, 9:10], col[:, 10:10 + K]
        ob = sb("ob", [2, D])
        nega = sb("nega", [P, 2])
        onesb = sb("onesb", [3, P], BF16)
        bb = wst[0:E, :, :].rearrange("p s f -> p (s f)")[:, 0:3 * (F + D)].rearrange("p (k f) -> p k f", k=3)
        bbp = crep[0:E, :, :].bitcast(BF16).rearrange("p h t -> p (h t)")[:, 0:3 * (F + D)].rearrange("p (k f) -> p k f", k=3)

        stats = sb("stats", [P, NB, 6])
        mv = sb("mv", [P, NB, 2])
        sm = sb("sm", [P, 12, NB])
        rt = hst[:, 2:5, :].rearrange("p u l -> p (u l)").rearrange("p (k e j) -> p k e j", k=6, e=E)
        first = sb("first", [P, E, NB])
        cnt = sb("cnt", [P, 6, E])
        cnti = sb("cnti", [P, E], I32)
        posi = sb("posi", [P, NB], I32)
        tilec = sb("tilec", [1, TILES, E])
        tcmp = y1[0:1, 0:TILES * E].rearrange("p (t e) -> p t e", e=E)
        tef = sb("tef", [1, TILES])
        tei = sb("tei", [1, TILES], I32)
        score = sb("score", [P, NB])
        zero = th

        bank = [ctx.enter_context(nc.psum_tensor(f"bank{i}", [P, 512], F32)) for i in range(8)]
        bank_d, bank_u, bank_y, bank_h, bank_m, bank_f = bank[0:2], bank[2:4], bank[4], bank[5], bank[6], bank[7]

        rows_in = nc.dram_tensor("rows_in", [TILES * P, D], F32, kind="Internal").ap()
        rows_out = nc.dram_tensor("rows_out", [TILES * P, D], F32, kind="Internal").ap()
        bias_parts = nc.dram_tensor("bias_parts", [E, 3, F + D], BF16, kind="Internal").ap()
        part_rows = nc.dram_tensor("part_rows", [D, 3, 2, L], BF16, kind="Internal").ap()

        x_in = [sem(f"x_in{c}") for c in range(CH)]
        consts_in = sem("consts_in")
        gate_in = sem("gate_in")
        rows_zeroed = sem("rows_zeroed")
        bias_stored = sem("bias_stored")
        scattered = sem("scattered")
        tile_x_in = [sem(f"tile_x_in{i}") for i in range(2)]
        tile_w1_in = [sem(f"tile_w1_in{i}") for i in range(2)]
        tile_w2_in = [sem(f"tile_w2_in{i}") for i in range(2)]
        ys_stored = [sem(f"ys_stored{i}") for i in range(2)]
        gathered = [sem(f"gathered{i}") for i in range(GAT)]
        parts_stored = sem("parts_stored")
        stack_in = sem("stack_in")
        out_stored = sem("out_stored")
        const_made = sem("const_made")
        zero_made = sem("zero_made")
        sel_made = sem("sel_made")
        expa_made = sem("expa_made")
        nega_made = sem("nega_made")
        gatew_made = sem("gatew_made")
        aggregated = sem("aggregated")
        score_made = sem("score_made")
        stat_made = sem("stat_made")
        small = sem("small")
        ln_made = sem("ln_made")
        rs_ready = sem("rs_ready")
        xn_made = sem("xn_made")
        xr_made = sem("xr_made")
        xt_turned = sem("xt_turned")
        xt_copied = sem("xt_copied")
        skip_made = sem("skip_made")
        gate_made = sem("gate_made")
        skip_added = sem("skip_added")
        inx_made = sem("inx_made")
        inres_made = sem("inres_made")
        xin_copied = sem("xin_copied")
        tap_made = sem("tap_made")
        conv_step = sem("conv_step")
        pad_made = sem("pad_made")
        xc_made = sem("xc_made")
        sres_made = sem("sres_made")
        low_made = sem("low_made")
        low_copied = sem("low_copied")
        dt_made = sem("dt_made")
        z_made = sem("z_made")
        e_made = sem("e_made")
        l_made = sem("l_made")
        delta_made = sem("delta_made")
        du_made = sem("du_made")
        route = sem("route")
        rexp_made = sem("rexp_made")
        rank_made = sem("rank_made")
        routed = sem("routed")
        bsplit = sem("bsplit")
        repd = sem("repd")
        repu = sem("repu")
        exped = sem("exped")
        mulb = sem("mulb")
        scanned = sem("scanned")
        pool_p = sem("pool_p")
        dve_p = sem("dve_p")
        reduced = sem("reduced")
        y1_made = sem("y1_made")
        yg_made = sem("yg_made")
        proj_made = sem("proj_made")
        acc_added = sem("acc_added")
        hi_made = sem("hi_made")
        rest_made = sem("rest_made")
        mid_made = sem("mid_made")
        lo_made = sem("lo_made")
        brep_mm = sem("brep_mm")
        brep_ready = sem("brep_ready")
        crep_mm = sem("crep_mm")
        crep_ready = sem("crep_ready")
        xs_turned = sem("xs_turned")
        xs_copied = sem("xs_copied")
        hidden = sem("hidden")
        tanh_made = sem("tanh_made")
        gated = sem("gated")
        down = sem("down")
        ys_copied = sem("ys_copied")
        combined = sem("combined")

        CONSTS = [(win, w_in), (wx, w_x), (wdt, w_dt), (wout, w_out), (wskip, w_skip), (col, cols),
                  (ob, out_b2), (strict, strict_in), (sel, None),
                  (red, red_in), (first, first_in), (tilec, tile_in)]
        x_blocks = x.rearrange("b (n p) d -> p (b n) d", p=P)
        out_blocks = out.rearrange("b (n p) d -> p (b n) d", p=P)

        BANKS, GROUPS, SLOTS = 2, 2, 2
        CREDITS = [(scanned, BANKS), (mulb, BANKS), (reduced, GROUPS), (down, SLOTS), (hidden, SLOTS), (xs_turned, SLOTS),
                   (gated, 1), (acc_added, 1),
                   (y1_made, 1), (ys_copied, 1), (pool_p, NP), (dve_p, ND), (ys_stored[0], 16), (ys_stored[1], 16)]

        def dd_of(c):
            if isinstance(c, int):
                return dd[:, c, :, :].rearrange("p w t -> p (w t)")
            return dd[:, bass.ds(c, 1), :, :].rearrange("p a w t -> p (a w t)")

        def row_of(tile, c):
            if isinstance(c, int):
                return tile[:, c, :]
            return tile[:, bass.ds(c, 1), :].rearrange("p a t -> p (a t)")

        def blocks_of(c):
            if isinstance(c, int):
                return acc[:, BPC * c:BPC * c + BPC, :]
            return acc[:, bass.ds(c * BPC, BPC), :]

        block = ctx.enter_context(nc.Block())

        @block.sync
        def _(sp):
            for credited, n in CREDITS:
                sp.sem_inc(credited, n)
            for c in range(CH):
                sp.dma_start(acc[:, BPC * c:BPC * c + BPC, :], x_blocks[:, BPC * c:BPC * c + BPC, :]).then_inc(x_in[c], 16)
                if c == 1:
                    sp.dma_start(ident[:, :], ident_in).then_inc(gate_in, 16)
                    sp.dma_start(wgate[:, :], w_gate).then_inc(gate_in, 16)
                    sp.dma_start(bb[:, 0, :], b1b2).then_inc(gate_in, 16)
            for dst, src in CONSTS:
                if src is None:
                    sp.dma_start(rest[:, 0:P], sel_in).then_inc(consts_in, 16)
                    continue
                sp.dma_start(dst[tuple(slice(None) for _ in dst.shape)], src).then_inc(consts_in, 16)
            sp.wait_ge(zero_made, 1)
            sp.dma_start(rows_in[0:TILES // 3 * P, :].rearrange("(n p) d -> p n d", p=P),
                         zero[:, 0:P].unsqueeze(1).broadcast_to([P, TILES // 3, P])).then_inc(rows_zeroed, 16)
            sp.dma_start(rows_in[TILES // 3 * P:2 * TILES // 3 * P, :].rearrange("(n p) d -> p n d", p=P),
                         zero[:, 0:P].unsqueeze(1).broadcast_to([P, TILES // 3, P])).then_inc(rows_zeroed, 16)
            sp.dma_start(rows_in[2 * TILES // 3 * P:, :].rearrange("(n p) d -> p n d", p=P),
                         zero[:, 0:P].unsqueeze(1).broadcast_to([P, TILES // 3, P])).then_inc(rows_zeroed, 16)
            sp.wait_ge(bsplit, 6)
            sp.dma_start(bias_parts, bbp[:, :, :]).then_inc(bias_stored, 16)

            def store_parts(c):
                sp.wait_ge(lo_made, c + 1)
                if not (isinstance(c, int) and c == 0):
                    sp.wait_ge(repd, UNITS * (c - 1) + 1)
                    sp.wait_ge(repu, UNITS * (c - 1) + 1)
                sp.dma_start(part_rows.rearrange("d k w t -> d (k w t)"),
                             parts[:, :, :].rearrange("p k t -> p (k t)")).then_inc(parts_stored, 16)

            def load_stack(c, h):
                sp.wait_ge(parts_stored, 16 * (c + 1))
                for q in range(QUADS):
                    rows = part_rows[32 * q:32 * q + 32].rearrange("(m e) k w t -> (e k) m (w t)", m=4)
                    sp.dma_start(stack[32 * q:32 * q + 3 * EC, h, :, :, :].rearrange("p m w t -> p m (w t)"),
                                 rows).then_inc(stack_in, 16)

            store_parts(0)
            load_stack(0, 0)
            sp.wait_ge(bias_stored, 16)
            sp.wait_ge(scattered, 16 * NB)
            sp.wait_ge(routed, 2)

            weights, biases = {}, {}

            def load_rows(b, i):
                t, s = b * TPB + i, i % 2
                sp.wait_ge(xs_turned, t + (1 if i else 2))
                sp.dma_start(xs[:, s, :], rows_in[bass.ds(t * P, P), :]).then_inc(tile_x_in[s], 16)

            def load_w1(b, i):
                t, s = b * TPB + i, i % 2
                e = sp.value_load(tei[0:1, bass.ds(t, 1)], min_val=0, max_val=E - 1)
                weights[i] = w_exp[bass.ds(e, 1)].rearrange("a p f -> p (a f)")
                biases[i] = bias_parts[bass.ds(e, 1)].rearrange("a k f -> k (a f)")
                sp.wait_ge(hidden, t + (1 if i else 2))
                sp.dma_start(wst[:, s, 0:F], weights[i][:, 0:F]).then_inc(tile_w1_in[s], 16)
                sp.dma_start(bst[:, s, 0:F], biases[i][:, 0:F]).then_inc(tile_w1_in[s], 16)

            def load_w2(b, i):
                t, s = b * TPB + i, i % 2
                sp.wait_ge(down, t + (1 if i else 2))
                sp.dma_start(wst[:, s, F:], weights[i][:, F:]).then_inc(tile_w2_in[s], 16)
                sp.dma_start(bst[:, s, F:], biases[i][:, F:]).then_inc(tile_w2_in[s], 16)

            def store_rows(b, i):
                t, s = b * TPB + i, i % 2
                sp.wait_ge(ys_copied, t + 1 + 1)
                sp.dma_start(rows_out[bass.ds(t * P, P), :], ysb[:, s, :]).then_inc(ys_stored[s], 16)

            def batch(b, last):
                for w in range(UB):
                    h, u = divmod(w, UNITS)
                    if not last:
                        if w == 0:
                            load_rows(b, 0)
                        for i in range(TPB):
                            if w == slot_down(i) - 6:
                                load_w1(b, i)
                                if i + 1 < TPB:
                                    load_rows(b, i + 1)
                            if w == slot_down(i) - 3:
                                load_w2(b, i)
                            if w == min(slot_down(i) + 1, UB - 1):
                                store_rows(b, i)
                    if not (last and h == HALVES - 1):
                        if u == SLOT_STORE:
                            store_parts(b * HALVES + h + 1)
                        if u == SLOT_STACK:
                            load_stack(b * HALVES + h + 1, (h + 1) % 2)

            with sp.Fori(0, B - 1) as b:
                batch(b, False)
            batch(B - 1, True)
            for c in range(CH):
                sp.wait_ge(combined, BPC * (c + 1))
                if c == CH - 1:
                    sp.wait_ge(acc_added, CH + 1)
                sp.dma_start(out_blocks[:, BPC * c:BPC * c + BPC, :], acc[:, BPC * c:BPC * c + BPC, :]).then_inc(out_stored, 16)
            sp.wait_ge(out_stored, 16 * CH)

        @block.gpsimd
        def _(pool):
            pool.memset(zero[:, :], 0.0).then_inc(zero_made, 1)
            pool.memset(ones[:, :], 1.0).then_inc(const_made, 1)
            pool.memset(onesb[:, :], 1.0).then_inc(const_made, 1)
            for c in range(CH):
                pool.wait_ge(small, 12)
                pool.wait_ge(xn_made, BPC * (c + 1))
                pool.tensor_tensor(xr[:, BPC * c:BPC * c + BPC, :], xn[c % 2],
                                   sm[:, 9, BPC * c:BPC * c + BPC].unsqueeze(2).broadcast_to([P, BPC, D]),
                                   ALU.mult).then_inc(xr_made, 1)
            pool.wait_ge(xr_made, CH)
            pool.wait_ge(rows_zeroed, 48)
            pool.wait_ge(routed, 1)
            for j in range(NB):
                pool.indirect_dma_start(out=rows_in[:, :], out_offset=bass.IndirectOffsetOnAxis(ap=posi[:, j:j + 1], axis=0),
                                        in_=xr[:, j, :], in_offset=None).then_inc(scattered, 16)

            def split_rest(c):
                pool.wait_ge(hi_made, c + 1)
                pool.tensor_tensor(rest[:, :], dd_of(c), parts[:, 0, :], ALU.subtract).then_inc(rest_made, 1)

            def split_lo(c):
                pool.wait_ge(mid_made, c + 1)
                pool.tensor_tensor(parts[:, 2, :], rest[:, :], parts[:, 1, :], ALU.subtract).then_inc(lo_made, 1)

            pool.wait_ge(sel_made, 1)
            split_rest(0)
            split_lo(0)

            def slot(b, w, first_one, last):
                h, u = divmod(w, UNITS)
                c = b * HALVES + h
                more = not (last and h == HALVES - 1)
                if u == SLOT_REST and more:
                    split_rest(c + 1)
                if u == SLOT_LO and more:
                    split_lo(c + 1)
                if w in (pool_last if last else pool_units):
                    pool.wait_ge(scanned, b * UB + w + 1 + BANKS)
                    pool.wait_ge(crep_ready, c + 1)
                    pool.wait_ge(reduced, 4 * c + u // 4 - 1 + GROUPS)
                    pool.tensor_tensor(ch_[:, u % RING_P, :], hst[:, u, :], crep[:, h, :], ALU.mult).then_inc(pool_p, 1)
                if last:
                    if w == HEAD:
                        for s in range(2):
                            pool.wait_ge(ys_stored[s], 16 * (((TPB + 1 - s) // 2) * (B - 1) + 1))
                    for j in gathers(w):
                        if j >= GAT:
                            pool.wait_ge(combined, j - GAT + 1)
                        pool.indirect_dma_start(out=gat[:, j % GAT, :], out_offset=None, in_=rows_out[:, :],
                                                in_offset=bass.IndirectOffsetOnAxis(ap=posi[:, j:j + 1], axis=0)
                                                ).then_inc(gathered[j % GAT], 16)

            batches(pool, slot)

        @block.scalar
        def _(act):
            def rsqrt_guess(n, src, lg, guess):
                act.wait_ge(small, n)
                act.activation(lg, src, ACT.Ln).then_inc(ln_made, 1)
                act.wait_ge(ln_made, 1 if n == 1 else 3)
                act.activation(guess, lg, ACT.Exp, scale=-0.5).then_inc(ln_made, 1)

            rsqrt_guess(1, sm[:, 0, :], sm[:, 1, :], sm[:, 2, :])
            rsqrt_guess(8, sm[:, 5, :], sm[:, 6, :], sm[:, 7, :])
            act.wait_ge(consts_in, 16 * len(CONSTS))
            act.activation(nega[:, 0:1], col[:, 5:6], ACT.Exp).then_inc(expa_made, 1)
            act.activation(sel[:, :], rest[:, 0:P], ACT.Copy).then_inc(sel_made, 1)
            for c in range(CH):
                act.wait_ge(xt_turned, c + 1)
                act.activation(dd[:, c, 1, :], bank[c % 2][:, :], ACT.Copy).then_inc(xt_copied, 1)
                act.wait_ge(inx_made, c + 1)
                if c >= 2:
                    act.wait_ge(conv_step, 3 * (c - 1))
                    act.wait_ge(pad_made, 1 + c // 2)
                act.activation(xin[c % 2][:, K - 1:], bank[5][:, :], ACT.Identity, bias=col[:, 0:1]).then_inc(xin_copied, 1)
                act.wait_ge(xin_copied, c + 1)
                if c >= 2:
                    act.wait_ge(xc_made, c - 1)
                act.activation(conv[c % 2], xin[c % 2][:, K - 1:], ACT.Identity, bias=col[:, 2:3],
                               scale=cw[:, K - 1:K]).then_inc(tap_made, 1)
                act.wait_ge(inres_made, c + 1)
                act.activation(sres[:, c, :], bank[6][:, :], ACT.Silu, bias=col[:, 1:2]).then_inc(sres_made, 1)
                if c >= 1:
                    act.wait_ge(conv_step, 3 * c)
                    act.activation(xc[:, c - 1, :], conv[(c - 1) % 2], ACT.Silu).then_inc(xc_made, 1)
            act.wait_ge(conv_step, 3 * CH)
            act.activation(xc[:, CH - 1, :], conv[(CH - 1) % 2], ACT.Silu).then_inc(xc_made, 1)
            act.wait_ge(route, 3)
            act.activation(rt[:, 1], rt[:, 0], ACT.Exp).then_inc(rexp_made, 1)

            def soft(c):
                act.wait_ge(z_made, c + 1)
                act.activation(soft_z[c % 2], soft_z[c % 2], ACT.Exp).then_inc(e_made, 1)
                act.wait_ge(e_made, c + 1)
                if c >= 2:
                    act.wait_ge(delta_made, c - 1)
                act.activation(soft_l[c % 2], soft_z[c % 2], ACT.Ln, bias=1.0).then_inc(l_made, 1)

            for c in range(CH):
                act.wait_ge(low_made, c + 1)
                if c >= 2:
                    act.wait_ge(dt_made, c - 1)
                act.activation(low[c % 2], bank[7][0:R, :], ACT.Identity, bias=lowb).then_inc(low_copied, 1)
                if c >= 1:
                    soft(c - 1)
            soft(CH - 1)

            def split_hi(c):
                act.wait_ge(du_made, CH)
                if not (isinstance(c, int) and c == 0):
                    act.wait_ge(parts_stored, 16 * c)
                act.activation(parts[:, 0, :], dd_of(c), ACT.Copy).then_inc(hi_made, 1)

            def split_mid(c):
                act.wait_ge(rest_made, c + 1)
                act.activation(parts[:, 1, :], rest[:, :], ACT.Copy).then_inc(mid_made, 1)

            def brep_copy(c, h):
                act.wait_ge(brep_mm, c + 1)
                if not (isinstance(c, int) and c == 0):
                    act.wait_ge(mulb, UNITS * (c - 1) + 1 + BANKS)
                act.activation(brep[:, h, :], bank_f[:, :], ACT.Identity, bias=col[:, 6:7]).then_inc(brep_ready, 1)

            def crep_copy(c, h):
                act.wait_ge(crep_mm, c + 1)
                if not (isinstance(c, int) and c == 0):
                    act.wait_ge(reduced, 4 * (c - 1) + GROUPS)
                act.activation(crep[:, h, :], bank_f[:, :], ACT.Identity, bias=col[:, 7:8]).then_inc(crep_ready, 1)

            def decay(b, w):
                act.wait_ge(repd, b * UB + w + 1)
                act.activation(bank_d[w % 2][:, :], bank_d[w % 2][:, :], ACT.Exp, scale=nega[:, 1:2]).then_inc(exped, 1)

            act.wait_ge(nega_made, 1)
            split_hi(0)
            brep_copy(0, 0)
            act.wait_ge(bias_stored, 16)
            crep_copy(0, 0)
            split_mid(0)
            decay(0, 0)
            decay(0, 1)

            def gain(b, i):
                act.wait_ge(xs_turned, b * TPB + i + 1 + SLOTS)
                act.activation(xsT[:, :], bank_m[:, 0:P], ACT.Copy, scale=rms).then_inc(xs_copied, 1)

            def half_tanh(b, i):
                t = b * TPB + i
                act.wait_ge(hidden, t + 1 + SLOTS)
                act.wait_ge(gated, t + 1)
                act.activation(th[:, :], bank_h[:, :], ACT.Tanh, scale=0.5).then_inc(tanh_made, 1)

            def copy_rows(b, i):
                t, s = b * TPB + i, i % 2
                act.wait_ge(down, t + 1 + SLOTS)
                act.wait_ge(ys_stored[s], 16 * (b * ((TPB + 1 - s) // 2) + i // 2 + 1))
                act.activation(ysb[:, s, :], bank_m[:, P:2 * P], ACT.Copy).then_inc(ys_copied, 1)

            def slot(b, w, first_one, last):
                h, u = divmod(w, UNITS)
                c = b * HALVES + h
                more = not (last and h == HALVES - 1)
                hn = (h + 1) % 2
                if w + AHEAD < UB:
                    decay(b, w + AHEAD)
                elif not last:
                    decay(b + 1, w + AHEAD - UB)
                if not last:
                    for i in range(TPB):
                        if w == slot_turn(i) and not i:
                            gain(b, i)
                        if w == slot_hidden(i):
                            half_tanh(b, i)
                        if w == slot_turn(i) and i:
                            gain(b, i)
                        if w == slot_down(i):
                            copy_rows(b, i)
                if more and u == SLOT_HI:
                    split_hi(c + 1)
                if more and u == SLOT_MID:
                    split_mid(c + 1)
                if more and u == SLOT_B:
                    brep_copy(c + 1, hn)
                if more and u == SLOT_C:
                    crep_copy(c + 1, hn)

            batches(act, slot)

        @block.vector
        def _(dve):
            steps = [0]

            def stat(ins):
                steps[0] += 1
                ins.then_inc(small, 1)
                dve.wait_ge(small, steps[0])

            dve.memset(xin[0][:, 0:K - 1], 0.0).then_inc(pad_made, 1)
            for j in range(NB):
                if j % BPC == 0:
                    dve.wait_ge(x_in[j // BPC], 16)
                dve.bn_stats(stats[:, j, :], acc[:, j, :]).then_inc(stat_made, 1)
            dve.wait_ge(stat_made, NB)
            for j in range(NB):
                dve.bn_aggr(mv[:, j, :], stats[:, j, :]).then_inc(aggregated, 1)
            dve.wait_ge(aggregated, NB)
            var = mv[:, :, 1]
            stat(dve.tensor_scalar(sm[:, 0, :], var, LN_EPS, None, ALU.add))

            def newton(value, guess, tmp, result):
                stat(dve.tensor_tensor(tmp, guess, guess, ALU.mult))
                stat(dve.tensor_tensor(tmp, tmp, value, ALU.mult))
                stat(dve.tensor_scalar(tmp, tmp, -0.5, 1.5, ALU.mult, ALU.add))
                stat(dve.tensor_tensor(result, guess, tmp, ALU.mult))

            dve.wait_ge(ln_made, 2)
            newton(sm[:, 0, :], sm[:, 2, :], sm[:, 3, :], sm[:, 4, :])
            stat(dve.tensor_tensor(sm[:, 8, :], var, sm[:, 4, :], ALU.mult))
            stat(dve.tensor_tensor(sm[:, 8, :], sm[:, 8, :], sm[:, 4, :], ALU.mult))
            stat(dve.tensor_scalar(sm[:, 5, :], sm[:, 8, :], RMS_EPS, None, ALU.add))

            def normalise(c):
                if c >= 2:
                    dve.wait_ge(xt_turned, c - 1)
                    dve.wait_ge(xr_made, c - 1)
                for j in range(BPC):
                    n = BPC * c + j
                    dve.tensor_scalar(xn[c % 2][:, j, :], acc[:, n, :], mv[:, n, 0:1], sm[:, 4, n:n + 1],
                                      ALU.subtract, ALU.mult).then_inc(xn_made, 1)

            normalise(0)
            dve.wait_ge(ln_made, 4)
            newton(sm[:, 5, :], sm[:, 7, :], sm[:, 3, :], sm[:, 9, :])
            normalise(1)
            dve.wait_ge(gate_in, 48)
            dve.wait_ge(consts_in, 16 * len(CONSTS))
            dve.tensor_scalar(wgate[:, :], wgate[:, :], rms, None, ALU.mult).then_inc(gatew_made, 1)
            made = [0]

            def bias(ins):
                made[0] += 1
                ins.then_inc(bsplit, 1)
                dve.wait_ge(bsplit, made[0])

            bias(dve.tensor_scalar(bb[:, 0, F:], bb[:, 0, F:], 2.0, None, ALU.mult))
            bias(dve.tensor_copy(bbp[:, 0, :], bb[:, 0, :]))
            bias(dve.tensor_tensor(bb[:, 1, :], bb[:, 0, :], bbp[:, 0, :], ALU.subtract))
            bias(dve.tensor_copy(bbp[:, 1, :], bb[:, 1, :]))
            bias(dve.tensor_tensor(bb[:, 2, :], bb[:, 1, :], bbp[:, 1, :], ALU.subtract))
            bias(dve.tensor_copy(bbp[:, 2, :], bb[:, 2, :]))
            dve.wait_ge(expa_made, 1)
            dve.tensor_scalar(nega[:, 1:2], nega[:, 0:1], -1.0, None, ALU.mult).then_inc(nega_made, 1)

            def convolve(c):
                if c % 2:
                    dve.wait_ge(xin_copied, c)
                    dve.tensor_copy(xin[1][:, 0:K - 1], xin[0][:, L:L + K - 1]).then_inc(pad_made, 1)
                    dve.wait_ge(pad_made, 2 + c // 2)
                dve.wait_ge(tap_made, c + 1)
                for n, k in enumerate(range(K - 2, -1, -1)):
                    if n:
                        dve.wait_ge(conv_step, 3 * c + n)
                    dve.scalar_tensor_tensor(out=conv[c % 2], in0=xin[c % 2][:, k:k + L], scalar=cw[:, k:k + 1],
                                             in1=conv[c % 2], op0=ALU.mult, op1=ALU.add).then_inc(conv_step, 1)

            for c in range(CH):
                dve.wait_ge(skip_made, c + 1)
                dve.tensor_tensor(acc[:, BPC * c:BPC * c + BPC, :], acc[:, BPC * c:BPC * c + BPC, :],
                                  bank[2 + c % 2][:, :].rearrange("p (j d) -> p j d", d=D), ALU.add).then_inc(skip_added, 1)
                if c + 2 < CH:
                    normalise(c + 2)
                convolve(c)

            done = [0]

            def step(ins):
                done[0] += 1
                ins.then_inc(route, 1)
                dve.wait_ge(route, done[0])

            def per_token(v):
                return v.unsqueeze(1).broadcast_to([P, E, NB])

            def by_token(v):
                return v.rearrange("p e j -> p j e")

            dve.wait_ge(gate_made, CH)
            step(dve.tensor_tensor(rt[:, 0], bank[4][:, 0:NB * E].rearrange("p (j e) -> p e j", e=E), per_token(sm[:, 9, :]), ALU.mult))
            step(dve.tensor_reduce(sm[:, 10, :], by_token(rt[:, 0]), AX_X, ALU.max))
            step(dve.tensor_tensor(rt[:, 0], rt[:, 0], per_token(sm[:, 10, :]), ALU.subtract))
            dve.wait_ge(rexp_made, 1)
            step(dve.tensor_reduce(sm[:, 11, :], by_token(rt[:, 1]), AX_X, ALU.add))
            step(dve.reciprocal(score[:, :], sm[:, 11, :]))
            step(dve.tensor_scalar(score[:, :], score[:, :], 0.5, None, ALU.mult))
            step(dve.scalar_tensor_tensor(out=rt[:, 2], in0=rt[:, 0], scalar=0.0, in1=first[:, :, :],
                                          op0=ALU.is_equal, op1=ALU.mult))
            step(dve.tensor_reduce(sm[:, 10, :], by_token(rt[:, 2]), AX_X, ALU.max))
            step(dve.tensor_tensor(rt[:, 3], rt[:, 2], per_token(sm[:, 10, :]), ALU.is_equal))
            one_hot = done[0]
            assert one_hot == 9
            dve.wait_ge(rank_made, 1)
            within = bank[2][:, 0:E * NB].rearrange("p (e j) -> p e j", e=E)
            total = bank[2][:, E * NB:2 * E * NB].rearrange("p (e j) -> p e j", e=E)
            for e in range(E):
                step(dve.tensor_tensor_scan(rt[:, 4, e, :], ones[:, 0:NB], total[:, e, :], 0.0, ALU.mult, ALU.add))
            step(dve.tensor_scalar(cnti[:, :], rt[:, 4, :, NB - 1], float(P - 1), None, ALU.add))
            step(dve.tensor_scalar(cnti[:, :], cnti[:, :], 7, 7, ALU.logical_shift_right, ALU.logical_shift_left))
            step(dve.tensor_copy(cnt[:, 1, :], cnti[:, :]))
            step(dve.tensor_tensor_scan(cnt[:, 2, :], ones[:, 0:E], cnt[:, 1, :], 0.0, ALU.mult, ALU.add))
            step(dve.tensor_tensor(cnt[:, 3, :], cnt[:, 2, :], cnt[:, 1, :], ALU.subtract))
            step(dve.tensor_tensor(rt[:, 5], within, rt[:, 4], ALU.add))
            step(dve.tensor_tensor(rt[:, 5], rt[:, 5], total, ALU.subtract))
            step(dve.tensor_tensor(rt[:, 5], rt[:, 5], cnt[:, 3, :].unsqueeze(2).broadcast_to([P, E, NB]), ALU.add))
            step(dve.tensor_tensor(rt[:, 5], rt[:, 5], rt[:, 3], ALU.mult))
            step(dve.tensor_reduce(sm[:, 10, :], by_token(rt[:, 5]), AX_X, ALU.add))
            dve.tensor_copy(posi[:, :], sm[:, 10, :]).then_inc(routed, 1)
            step(dve.tensor_tensor(tcmp[:, :, :], tilec[:, :, :], cnt[0:1, 2, :].unsqueeze(1).broadcast_to([1, TILES, E]), ALU.is_ge))
            step(dve.tensor_reduce(tef[:, :], tcmp[:, :, :], AX_X, ALU.add))
            dve.tensor_scalar(tei[:, :], tef[:, :], float(E - 1), None, ALU.min).then_inc(routed, 1)

            def cut(c):
                dve.wait_ge(dt_made, c + 1)
                if c >= 2:
                    dve.wait_ge(l_made, c - 1)
                dve.tensor_scalar(soft_z[c % 2], bank[c % 2][:, :], col[:, 3:4], SOFTPLUS_CUT, ALU.add, ALU.min).then_inc(z_made, 1)

            cut(0)
            for c in range(CH):
                if c + 1 < CH:
                    cut(c + 1)
                dve.wait_ge(l_made, c + 1)
                dve.scalar_tensor_tensor(out=dd[:, c, 0, :], in0=bank[c % 2][:, :], scalar=col[:, 3:4], in1=soft_l[c % 2],
                                         op0=ALU.add, op1=ALU.max).then_inc(delta_made, 1)
                if c >= 1:
                    dve.wait_ge(delta_made, c)
                    dve.tensor_tensor(dd[:, c - 1, 1, :], dd[:, c - 1, 0, :], xc[:, c - 1, :], ALU.mult).then_inc(du_made, 1)
            dve.wait_ge(delta_made, CH)
            dve.tensor_tensor(dd[:, CH - 1, 1, :], dd[:, CH - 1, 0, :], xc[:, CH - 1, :], ALU.mult).then_inc(du_made, 1)

            def drive(b, w):
                h, u = divmod(w, UNITS)
                dve.wait_ge(repu, b * UB + w + 1)
                dve.wait_ge(brep_ready, b * HALVES + h + 1)
                dve.tensor_tensor(dbu[:, w % RING_B, :], bank_u[w % 2][:, :], brep[:, h, :], ALU.mult).then_inc(mulb, 1)

            def scan(b, w, last):
                h, u = divmod(w, UNITS)
                dve.wait_ge(exped, b * UB + w + 1)
                dve.wait_ge(mulb, b * UB + w + 1 + BANKS)
                v, units_p, units_d = (w - UNITS, pool_last, DVE_P_LAST) if last and w >= UNITS else (w - UNITS, pool_units, DVE_P)
                back = 0 if v >= 0 else 1
                v %= UB
                if v in units_d:
                    dve.wait_ge(dve_p, (b - back) * ND + before(units_d, v) + 1 + ND)
                else:
                    dve.wait_ge(pool_p, (b - back) * NP + before(units_p, v) + 1 + NP)
                if w == UNITS // 2:
                    dve.wait_ge(scattered, 16 * NB)
                start = hst[:, u, L - 1:L] if h else 0.0
                dve.tensor_tensor_scan(hst[:, u, :], bank_d[w % 2][:, :], dbu[:, w % RING_B, :], start,
                                       ALU.mult, ALU.add).then_inc(scanned, 1)

            drive(0, 0)
            drive(0, 1)

            def combine(j):
                dve.wait_ge(gathered[j % GAT], 16 * (j // GAT + 1))
                dve.scalar_tensor_tensor(out=acc[:, j, :], in0=gat[:, j % GAT, :], scalar=score[:, j:j + 1],
                                         in1=acc[:, j, :], op0=ALU.mult, op1=ALU.add).then_inc(combined, 1)

            def add_skip(c):
                dve.wait_ge(reduced, 4 * (c + 1) + GROUPS)
                dve.scalar_tensor_tensor(out=y1[:, :], in0=row_of(xc, c), scalar=col[:, 4:5], in1=bank_y[:, :],
                                         op0=ALU.mult, op1=ALU.add).then_inc(y1_made, 1)

            def gate_sum(c):
                dve.wait_ge(y1_made, c + 1 + 1)
                dve.wait_ge(proj_made, c)
                dve.tensor_tensor(yg[:, :], y1[:, :], row_of(sres, c), ALU.mult).then_inc(yg_made, 1)

            def add_projection(c):
                dve.wait_ge(proj_made, c + 1)
                dve.tensor_tensor(blocks_of(c), blocks_of(c), bank_f[:, :].rearrange("p (j d) -> p j d", d=D),
                                  ALU.add).then_inc(acc_added, 1)

            def slot(b, w, first_one, last):
                h, u = divmod(w, UNITS)
                c = b * HALVES + h
                scan(b, w, last)
                ends = u < HEAD and not (first_one and h == 0)
                if ends and u == 2:
                    gate_sum(c - 1)
                if w + AHEAD < UB:
                    drive(b, w + AHEAD)
                elif not last:
                    drive(b + 1, w + AHEAD - UB)
                if last:
                    for j in gathers(w - 2):
                        combine(j)
                if w in (DVE_P_LAST if last else DVE_P):
                    dve.wait_ge(scanned, b * UB + w + 1 + BANKS)
                    dve.wait_ge(crep_ready, c + 1)
                    dve.wait_ge(reduced, 4 * c + u // 4 - 1 + GROUPS)
                    dve.tensor_tensor(ch_[:, u % RING_P, :], hst[:, u, :], crep[:, h, :], ALU.mult).then_inc(dve_p, 1)
                if not last:
                    for i in range(TPB):
                        if w == slot_gate(i):
                            t = b * TPB + i
                            dve.wait_ge(tanh_made, t + 1)
                            dve.wait_ge(down, t + (1 if i else 2))
                            dve.scalar_tensor_tensor(out=hid[:, i % 2, :], in0=th[:, :], scalar=1.0, in1=bank_h[:, :],
                                                     op0=ALU.add, op1=ALU.mult).then_inc(gated, 1)
                if ends and u == 1:
                    add_skip(c - 1)
                if ends and u == 3:
                    add_projection(c - 1)

            batches(dve, slot)
            for w in (UB - 2, UB - 1):
                for j in gathers(w):
                    combine(j)
            add_skip(CH - 1)
            gate_sum(CH - 1)
            dve.wait_ge(combined, NB)
            add_projection(CH - 1)

        @block.tensor
        def _(pe):
            def turn(c):
                pe.wait_ge(xn_made, BPC * (c + 1))
                if c >= 2:
                    pe.wait_ge(xt_copied, c - 1)
                for j in range(BPC):
                    mm = pe.transpose(bank[c % 2][:, P * j:P * j + P], xn[c % 2][:, j, :], ident[:, :])
                mm.then_inc(xt_turned, 1)

            pe.wait_ge(gate_in, 48)
            turn(0)
            for c in range(CH):
                if c + 1 < CH:
                    turn(c + 1)
                if c == 0:
                    pe.wait_ge(consts_in, 16 * len(CONSTS))
                    pe.wait_ge(const_made, 2)
                    pe.wait_ge(gatew_made, 1)
                pe.wait_ge(xt_copied, c + 1)
                xt = dd[:, c, 1, :]
                if c >= 1:
                    pe.wait_ge(xin_copied, c)
                pe.matmul(bank[5][:, :], win[:, 0:D], xt, start=True, stop=True).then_inc(inx_made, 1)
                if c >= 1:
                    pe.wait_ge(sres_made, c)
                pe.matmul(bank[6][:, :], win[:, D:2 * D], xt, start=True, stop=True).then_inc(inres_made, 1)
                if c >= 2:
                    pe.wait_ge(skip_added, c - 1)
                for j in range(BPC):
                    o = bank[2 + c % 2][:, P * j:P * j + P]
                    pe.matmul(o, ones[0:2, :], ob[:, :], start=True, stop=False)
                    mm = pe.matmul(o, xt[:, P * j:P * j + P], wskip[:, :], start=False, stop=True)
                mm.then_inc(skip_made, 1)
                for j in range(BPC):
                    n = BPC * c + j
                    mm = pe.matmul(bank[4][:, E * n:E * n + E], xt[:, P * j:P * j + P], wgate[:, :], start=True, stop=True)
                mm.then_inc(gate_made, 1)
            pe.wait_ge(route, 9)
            pe.wait_ge(skip_added, CH)
            pe.matmul(bank[2][:, 0:E * NB], strict[:, :], rt[:, 3].rearrange("p e j -> p (e j)"), start=True, stop=True)
            pe.matmul(bank[2][:, E * NB:2 * E * NB], ones[:, :], rt[:, 3].rearrange("p e j -> p (e j)"),
                      start=True, stop=True).then_inc(rank_made, 1)

            def low_rank(c):
                pe.wait_ge(xc_made, c + 1)
                if c >= 1:
                    pe.wait_ge(low_copied, c)
                pe.matmul(bank[7][0:R, :], wx[:, 0:R], xc[:, c, :], start=True, stop=True).then_inc(low_made, 1)

            low_rank(0)
            for c in range(CH):
                if c + 1 < CH:
                    low_rank(c + 1)
                pe.wait_ge(low_copied, c + 1)
                if c >= 2:
                    pe.wait_ge(delta_made, c - 1)
                pe.matmul(bank[c % 2][:, :], wdt[:, :], low[c % 2], start=True, stop=True).then_inc(dt_made, 1)

            def brep_matmul(c):
                if isinstance(c, int) and c == 0:
                    pe.wait_ge(low_copied, CH)
                else:
                    pe.wait_ge(acc_added, c - 1 + 1)
                pe.matmul(bank_f[:, :], wx[:, R:R + P], row_of(xc, c), start=True, stop=True).then_inc(brep_mm, 1)

            def crep_matmul(c):
                pe.wait_ge(brep_ready, c + 1)
                pe.matmul(bank_f[:, :], wx[:, R + P:R + 2 * P], row_of(xc, c), start=True, stop=True).then_inc(crep_mm, 1)

            def rep_u(b, w):
                h, u = divmod(w, UNITS)
                m, q = divmod(u, QUADS)
                if u == 0:
                    pe.wait_ge(stack_in, 16 * QUADS * (b * HALVES + h + 1))
                pe.wait_ge(mulb, b * UB + w - 1 + BANKS)
                rows = slice(32 * q, 32 * q + 3 * EC)
                pe.matmul(bank_u[w % 2][:, :], sel[rows, :], stack[rows, h, m, 1, :], start=True, stop=True,
                          tile_position=(32 * q, 0)).then_inc(repu, 1)

            def rep_d(b, w):
                h, u = divmod(w, UNITS)
                m, q = divmod(u, QUADS)
                pe.wait_ge(scanned, b * UB + w - 1 + BANKS)
                rows = slice(32 * q, 32 * q + 3 * EC)
                pe.matmul(bank_d[w % 2][:, :], sel[rows, :], stack[rows, h, m, 0, :], start=True, stop=True,
                          tile_position=(32 * q, 0)).then_inc(repd, 1)

            brep_matmul(0)
            crep_matmul(0)
            pe.wait_ge(du_made, CH)
            pe.wait_ge(routed, 2)
            pe.wait_ge(sel_made, 1)
            for w in range(AHEAD):
                rep_u(0, w)
                rep_d(0, w)
            rep_u(0, AHEAD)

            def reduce(b, h, m, last):
                c = b * HALVES + h
                end = h * UNITS + 4 * m + 4
                units_p, units_d = (pool_last, DVE_P_LAST) if last else (pool_units, DVE_P)
                pe.wait_ge(pool_p, b * NP + before(units_p, end) + NP)
                pe.wait_ge(dve_p, b * ND + before(units_d, end) + ND)
                if m == 0:
                    pe.wait_ge(y1_made, c + 1)
                for q in range(QUADS):
                    mm = pe.matmul(bank_y[32 * q:32 * q + 32, :], red[:, m, :], ch_[:, (4 * m + q) % RING_P, :],
                                   start=(m == 0), stop=(m == 3), tile_position=(0, 32 * q))
                mm.then_inc(reduced, 1)

            def project(c):
                pe.wait_ge(yg_made, c + 1)
                pe.wait_ge(crep_ready, c + 2 if not isinstance(c, int) or c < CH - 1 else CH)
                for j in range(BPC):
                    mm = pe.matmul(bank_f[:, P * j:P * j + P], yg[:, P * j:P * j + P], wout[:, :], start=True, stop=True)
                mm.then_inc(proj_made, 1)

            def turn_rows(b, i):
                t, s = b * TPB + i, i % 2
                pe.wait_ge(tile_x_in[s], 16 * (b * ((TPB + 1 - s) // 2) + i // 2 + 1))
                pe.wait_ge(ys_copied, t + 1 - min(i, 2))
                pe.transpose(bank_m[:, 0:P], xs[:, s, :], ident[:, :]).then_inc(xs_turned, 1)

            def make_hidden(b, i):
                t, s = b * TPB + i, i % 2
                pe.wait_ge(tile_w1_in[s], 32 * (b * ((TPB + 1 - s) // 2) + i // 2 + 1))
                pe.wait_ge(xs_copied, t + 1)
                pe.wait_ge(gated, t + 1)
                for f in range(FC):
                    o = bank_h[:, P * f:P * f + P]
                    pe.matmul(o, bst[:, s, P * f:P * f + P], onesb[:, :], start=True, stop=False)
                    mm = pe.matmul(o, wst[:, s, P * f:P * f + P], xsT[:, :], start=False, stop=True)
                mm.then_inc(hidden, 1)

            def make_down(b, i):
                t, s = b * TPB + i, i % 2
                pe.wait_ge(tile_w2_in[s], 32 * (b * ((TPB + 1 - s) // 2) + i // 2 + 1))
                pe.wait_ge(ys_copied, t + 1)
                pe.wait_ge(xs_copied, t + 1 + min(2, TPB - 1 - i))
                pe.wait_ge(gated, t + 1 + 1)
                pe.matmul(bank_m[:, P:2 * P], onesb[:, :], bst[:, s, F:F + D], start=True, stop=False)
                for f in range(FC):
                    mm = pe.matmul(bank_m[:, P:2 * P], hid[:, s, P * f:P * f + P],
                                   wst[:, s, F + D * f:F + D * f + D], start=False, stop=(f == FC - 1))
                mm.then_inc(down, 1)

            def slot(b, w, first_one, last):
                h, u = divmod(w, UNITS)
                c = b * HALVES + h
                more = not (last and h == HALVES - 1)
                ends = u < HEAD and not (first_one and h == 0)
                for ahead, rep in ((AHEAD, rep_d), (AHEAD + 1, rep_u)):
                    if w + ahead < UB:
                        rep(b, w + ahead)
                    elif not last:
                        rep(b + 1, w + ahead - UB)
                if more and u == SLOT_B:
                    brep_matmul(c + 1)
                if more and u == SLOT_C:
                    crep_matmul(c + 1)
                if u in (6, 10, 14):
                    reduce(b, h, (u - 6) // 4, last)
                if ends and u == 0:
                    if h:
                        reduce(b, h - 1, 3, last)
                    else:
                        reduce(b - 1, HALVES - 1, 3, last)
                if ends and u == 2:
                    project(c - 1)
                if not last:
                    if w == HEAD:
                        turn_rows(b, 0)
                    for i in range(TPB):
                        if w == slot_hidden(i):
                            make_hidden(b, i)
                        if w == slot_down(i):
                            make_down(b, i)
                    for i in range(TPB):
                        if w == slot_turn(i) and i:
                            turn_rows(b, i)

            batches(pe, slot)
            reduce(B - 1, HALVES - 1, 3, True)
            project(CH - 1)


def kernel(**inputs):
    import numpy as np
    import concourse.bacc as bacc
    from concourse.bass_utils import run_bass_kernel_spmd as run

    a = {k: np.asarray(v) for k, v in inputs.items()}
    at = lambda n: a["L0_attn_" + n]
    ff = lambda n: a["L0_ffn_" + n]
    xp = at("x_proj_w").T
    xb = at("x_proj_b")
    cols = np.stack([at("in_proj_b")[:D], at("in_proj_b")[D:], at("conv_b"), at("dt_proj_b"), at("D_param"),
                     np.repeat(at("A_log")[0], EC), np.repeat(xb[R:R + N], EC), np.repeat(xb[R + N:], EC),
                     np.concatenate([xb[:R], xb[:R]]), ff("rms_w")] + [at("conv_w")[:, 0, k] for k in range(K)], axis=1)
    w1 = ff("W1")
    w2 = ff("W2").reshape(E, FC, P, D).transpose(0, 2, 1, 3).reshape(E, P, FC * D)
    n = np.arange(P)
    sel = np.zeros((P, P), np.float32)
    for q in range(QUADS):
        for e in range(EC):
            for k in range(3):
                sel[32 * q + 3 * e + k, e::EC] = 1.0
    red = np.zeros((P, 4, 32), np.float32)
    for m in range(4):
        red[n, m, EC * m + n % EC] = 1.0
    arrays = {
        "x": at("x"), "w_in": at("in_proj_w").T,
        "w_x": np.concatenate([xp[:, :R], np.repeat(xp[:, R:R + N], EC, axis=1), np.repeat(xp[:, R + N:], EC, axis=1)], axis=1),
        "w_dt": at("dt_proj_w").T, "w_out": at("out_proj_w").T, "w_skip": at("skip_proj_w").T, "w_gate": ff("gate_w").T,
        "w_exp": np.concatenate([w1, w2], axis=2), "b1b2": np.concatenate([ff("b1"), ff("b2")], axis=1),
        "cols": cols,
        "out_b2": np.stack([at("out_proj_b"), at("skip_proj_b")]),
        "ident": np.eye(P, dtype=np.float32), "strict": np.triu(np.ones((P, P), np.float32), 1), "sel": sel, "red": red,
        "first": np.ascontiguousarray(np.broadcast_to((E - np.arange(E, dtype=np.float32))[None, :, None], (P, E, NB))),
        "tiles": np.ascontiguousarray(np.broadcast_to((P * np.arange(TILES, dtype=np.float32))[None, :, None], (1, TILES, E))),
    }
    nc = bacc.Bacc("TRN2", target_bir_lowering=False, num_devices=1)
    arrays = {f"in_{k}_dram": np.ascontiguousarray(v) for k, v in arrays.items()}
    args = [nc.dram_tensor(k, v.shape, mybir.dt.from_np(v.dtype), kind="ExternalInput").ap() for k, v in arrays.items()]
    args.append(nc.dram_tensor("out_0_dram", (B, T, D), F32, kind="ExternalOutput").ap())
    block_program(nc, *args)
    r = run(nc, [arrays], core_ids=[0])
    return r.results[0]["out_0_dram"]
```

```python
from contextlib import ExitStack

import concourse.bass as bass
from concourse import mybir

F32 = mybir.dt.float32
BF16 = mybir.dt.bfloat16
I32 = mybir.dt.int32
ALU = mybir.AluOpType
ACT = mybir.ActivationFunctionType
AX_X = mybir.AxisListType.X

P = 128
B, T, D = 4, 1024, 128
N = 16
K = 4
R = 64
E, F = 8, 512
L = 512
HALVES = T // L
CH = B * HALVES
BPC = L // P
NB = CH * BPC
EC = P // N
UNITS = D // EC
UB = UNITS * HALVES
QUADS = 4
FC = F // P
TILES = NB + E - 1
TPB = TILES // (B - 1)
assert TPB * (B - 1) == TILES
LN_EPS, RMS_EPS = 1e-5, 1e-6
SOFTPLUS_CUT = 30.0
ROOT_MAGIC = float(0x5F3759DF)
RING_B, RING_P = 4, 8
GAT = 4 * F // P
AHEAD = 2
HEAD = 4
assert HEAD <= UNITS

DVE_P = {15, 31}
DVE_P_LAST = {15, 31, 14, 30, 5, 7, 9, 11, 13, 17, 19, 21, 23, 25, 27, 29}
assert all(w >= HEAD for w in DVE_P | DVE_P_LAST)


SLOT_HIDDEN = (4, 6, 8, 10, 12, 14, 17, 20, 22, 24, 26, 29, 32)
SLOT_DOWN = (7, 9, 11, 13, 15, 19, 21, 23, 25, 27, 30, 33, 35)
SLOT_TURN = (HEAD,) + SLOT_HIDDEN[:-1]
SLOT_GATE = SLOT_HIDDEN[1:] + (34,)
assert len(SLOT_HIDDEN) == len(SLOT_DOWN) == TPB and max(SLOT_DOWN) < UB + HEAD


def tiles_at(slots, b, w, first_one, last):
    if w < HEAD:
        return [] if first_one else [(b - 1, i) for i in range(TPB) if slots[i] == w + UB]
    return [] if last else [(b, i) for i in range(TPB) if slots[i] == w]


SLOT_HI, SLOT_REST, SLOT_MID, SLOT_LO, SLOT_STORE, SLOT_STACK = 0, 1, 3, 4, 6, 8
SLOT_B, SLOT_C = (4, 5), (5, 9)
SLOTS_SUM = (6, 11, 14)
SLOT_SUM_LAST, SLOT_PROJECT = 0, 2


def batches(engine, slot):
    for w in range(HEAD):
        slot(0, w, True, False)
    with engine.Fori(0, B - 1) as b:
        for w in range(HEAD, UB):
            slot(b, w, False, False)
        for w in range(HEAD):
            slot(b + 1, w, False, False)
    for w in range(HEAD, UB):
        slot(B - 1, w, False, True)


FIRST_GATHER, EXTRA_GATHER, GATHER_LAG = 5, 17, 5


def gathers(w):
    def until(v):
        return min(NB, sum(1 + (x in DVE_P_LAST and x >= EXTRA_GATHER) for x in range(FIRST_GATHER, v)))
    return list(range(until(w), until(w + 1)))


def combines(w):
    def until(v):
        return min(NB, sum(len(gathers(x)) for x in range(0, v - GATHER_LAG)))
    return list(range(until(w), until(w + 1)))


def before(units, w):
    return sum(1 for x in units if x < w)


def block_program(nc, x, w_in, w_x, w_dt, w_out, w_skip, w_gate, w_exp, b1b2, cols, out_b2,
                  ident_in, strict_in, sel_in, blocksel_in, red_in, first_in, tile_in, out):
    pool_units = [w for w in range(UB) if w not in DVE_P]
    pool_last = [w for w in range(UB) if w not in DVE_P_LAST]
    NP, ND = len(pool_units), len(DVE_P)

    with ExitStack() as ctx:
        def sb(name, shape, dt=F32):
            return ctx.enter_context(nc.sbuf_tensor(name, shape, dt))

        def sem(name):
            return ctx.enter_context(nc.semaphore(name))

        acc = sb("acc", [P, NB, D])
        dd = sb("dd", [P, CH, 2, L])
        xc = sb("xc", [P, CH, L])
        sres = sb("sres", [P, CH, L])
        hst = sb("hst", [P, UNITS, L])
        xr = hst[:, UNITS // 2:UNITS, :].rearrange("p u (j d) -> p (u j) d", d=D)
        dbu = sb("dbu", [P, RING_B, L])
        ch_ = sb("ch", [P, RING_P, L])
        brep = sb("brep", [P, HALVES, L])
        crep = sb("crep", [P, HALVES, L])
        parts = sb("parts", [P, 3, 2 * L], BF16)
        rest = sb("rest", [P, 2 * L])
        stack = sb("stack", [P, HALVES, 4, 2, L], BF16)
        y1 = sb("y1", [P, L])
        yg = sb("yg", [P, L])
        wst = sb("wst", [P, 2, 2 * F])
        b1st = sb("b1st", [3 * FC, 2, P], BF16)
        b2st = sb("b2st", [3, 2, D], BF16)
        blocksel = sb("blocksel", [3 * FC, F], BF16)
        xs = sb("xs", [P, 2, D])
        xsT = sb("xsT", [P, P])
        th = sb("th", [P, F])
        hid = sb("hid", [P, 2, F])
        ysb = sb("ysb", [P, 2, D])
        xin = [dbu[:, 0:2, :].rearrange("p a l -> p (a l)")[:, 0:L + K - 1],
               dbu[:, 2:4, :].rearrange("p a l -> p (a l)")[:, 0:L + K - 1]]
        xn = xr
        conv = [ch_[:, i, :] for i in range(2)]
        low = [ch_[0:R, 2 + i, :] for i in range(2)]
        gat = wst[:, :, :].rearrange("p s (j d) -> p (s j) d", d=D)

        ident = sb("ident", [P, P])
        strict = sb("strict", [P, P])
        ones = sb("ones", [P, P])
        sel = sb("sel", [P, P], BF16)
        red = sb("red", [P, 4, 32])
        win = sb("win", [P, 2 * D])
        wx = sb("wx", [P, R + 2 * P])
        wdt = sb("wdt", [R, D])
        wout = sb("wout", [P, D])
        wsg = sb("wsg", [P, D + E])
        col = sb("col", [P, 10 + K])
        lowb, rms, cw = col[0:R, 8:9], col[:, 9:10], col[:, 10:10 + K]
        ob = sb("ob", [2, D])
        bias_rep = sb("bias_rep", [P, D])
        nega = sb("nega", [P, 2])
        onesb = sb("onesb", [3, P], BF16)
        bb = wst[0:E, :, :].rearrange("p s f -> p (s f)")[:, 0:3 * (F + D)].rearrange("p (k f) -> p k f", k=3)
        bbp = crep[0:E, :, :].bitcast(BF16).rearrange("p h t -> p (h t)")[:, 0:3 * (F + D)].rearrange("p (k f) -> p k f", k=3)

        stats = sb("stats", [P, NB, 6])
        mv = sb("mv", [P, NB, 2])
        sm = sb("sm", [P, 12, NB])
        rt = hst[:, 2:5, :].rearrange("p u l -> p (u l)").rearrange("p (k e j) -> p k e j", k=6, e=E)
        first = sb("first", [P, E, NB])
        cnt = sb("cnt", [P, 6, E])
        cnti = sb("cnti", [P, E], I32)
        posi = sb("posi", [P, NB], I32)
        tilec = yg[0:1, 0:TILES * E].rearrange("p (t e) -> p t e", e=E)
        tcmp = y1[0:1, 0:TILES * E].rearrange("p (t e) -> p t e", e=E)
        tef = sb("tef", [1, TILES])
        tei = sb("tei", [1, TILES], I32)
        score = sb("score", [P, NB])
        logits = rt[:, 5].rearrange("p e j -> p (e j)").rearrange("p (j e) -> p j e", e=E)
        zero = th

        bank = [ctx.enter_context(nc.psum_tensor(f"bank{i}", [P, 512], F32)) for i in range(8)]
        bank_d, bank_u, bank_y, bank_h, bank_m, bank_f = bank[0:2], bank[2:4], bank[4], bank[5], bank[6], bank[7]

        rows_in = nc.dram_tensor("rows_in", [TILES * P, D], F32, kind="Internal").ap()
        rows_out = nc.dram_tensor("rows_out", [TILES * P, D], F32, kind="Internal").ap()
        bias_parts = nc.dram_tensor("bias_parts", [E, 3, F + D], BF16, kind="Internal").ap()
        part_rows = nc.dram_tensor("part_rows", [D, 3, 2, L], BF16, kind="Internal").ap()

        x_in = [sem(f"x_in{c}") for c in range(CH)]
        consts_in = sem("consts_in")
        gate_in = sem("gate_in")
        proj_in = sem("proj_in")
        rows_zeroed = sem("rows_zeroed")
        bias_stored = sem("bias_stored")
        scattered = sem("scattered")
        tile_x_in = [sem(f"tile_x_in{i}") for i in range(2)]
        tile_w1_in = [sem(f"tile_w1_in{i}") for i in range(2)]
        tile_w2_in = [sem(f"tile_w2_in{i}") for i in range(2)]
        ys_stored = [sem(f"ys_stored{i}") for i in range(2)]
        gathered = [sem(f"gathered{i}") for i in range(GAT)]
        parts_stored = sem("parts_stored")
        stack_in = sem("stack_in")
        out_stored = sem("out_stored")
        const_made = sem("const_made")
        zero_made = sem("zero_made")
        sel_made = sem("sel_made")
        expa_made = sem("expa_made")
        nega_made = sem("nega_made")
        gatew_made = sem("gatew_made")
        aggregated = sem("aggregated")
        score_made = sem("score_made")
        stat_made = sem("stat_made")
        small = sem("small")
        rms_ready = sem("rms_ready")
        bias_mm = sem("bias_mm")
        bias_ready = sem("bias_ready")
        bias_added = sem("bias_added")
        xn_made = sem("xn_made")
        xr_made = sem("xr_made")
        xt_turned = sem("xt_turned")
        xt_copied = sem("xt_copied")
        skip_made = sem("skip_made")
        gate_made = sem("gate_made")
        skip_added = sem("skip_added")
        inx_made = sem("inx_made")
        inres_made = sem("inres_made")
        xin_copied = sem("xin_copied")
        tap_made = sem("tap_made")
        conv_step = sem("conv_step")
        pad_made = sem("pad_made")
        xc_made = sem("xc_made")
        sres_made = sem("sres_made")
        low_made = sem("low_made")
        low_copied = sem("low_copied")
        dt_made = sem("dt_made")
        x_made = sem("x_made")
        z_made = sem("z_made")
        e_made = sem("e_made")
        l_made = sem("l_made")
        delta_made = sem("delta_made")
        du_made = sem("du_made")
        route = sem("route")
        rexp_made = sem("rexp_made")
        rank_made = sem("rank_made")
        routed = sem("routed")
        bsplit = sem("bsplit")
        repd = sem("repd")
        repu = sem("repu")
        exped = sem("exped")
        mulb = sem("mulb")
        scanned = sem("scanned")
        pool_p = sem("pool_p")
        dve_p = sem("dve_p")
        reduced = sem("reduced")
        y1_made = sem("y1_made")
        yg_made = sem("yg_made")
        proj_made = sem("proj_made")
        acc_added = sem("acc_added")
        hi_made = sem("hi_made")
        rest_made = sem("rest_made")
        mid_made = sem("mid_made")
        lo_made = sem("lo_made")
        brep_mm = sem("brep_mm")
        brep_ready = sem("brep_ready")
        crep_mm = sem("crep_mm")
        crep_ready = sem("crep_ready")
        xs_turned = sem("xs_turned")
        xs_copied = sem("xs_copied")
        hidden = sem("hidden")
        tanh_made = sem("tanh_made")
        gated = sem("gated")
        down = sem("down")
        ys_copied = sem("ys_copied")
        combined = sem("combined")

        GATE_CONSTS = [(ident, ident_in), (wsg[:, D:], w_gate), (col, cols)]
        PROJ_CONSTS = [(win, w_in), (wsg[:, 0:D], w_skip), (ob, out_b2)]
        CONSTS = [(bb[:, 0, :], b1b2), (wx, w_x), (wdt, w_dt), (wout, w_out), (strict, strict_in), (rest[:, 0:P], sel_in),
                  (rest[0:3 * FC, P:P + F], blocksel_in),
                  (red, red_in), (first, first_in), (tilec, tile_in)]
        x_blocks = x.rearrange("b (n p) d -> p (b n) d", p=P)
        out_blocks = out.rearrange("b (n p) d -> p (b n) d", p=P)

        BANKS, GROUPS, SLOTS = 2, 2, 2
        CREDITS = [(scanned, BANKS), (mulb, BANKS), (reduced, GROUPS), (down, SLOTS), (hidden, SLOTS), (xs_turned, SLOTS),
                   (gated, 1), (acc_added, 2),
                   (y1_made, 1), (ys_copied, 1), (pool_p, NP), (dve_p, ND), (ys_stored[0], 16), (ys_stored[1], 16)]

        def dd_of(c):
            if isinstance(c, int):
                return dd[:, c, :, :].rearrange("p w t -> p (w t)")
            return dd[:, bass.ds(c, 1), :, :].rearrange("p a w t -> p (a w t)")

        def row_of(tile, c):
            if isinstance(c, int):
                return tile[:, c, :]
            return tile[:, bass.ds(c, 1), :].rearrange("p a t -> p (a t)")

        def skip_banks(c):
            return (4, 7) if c % 2 else (2, 3)

        def blocks_of(c):
            if isinstance(c, int):
                return acc[:, BPC * c:BPC * c + BPC, :]
            return acc[:, bass.ds(c * BPC, BPC), :]

        block = ctx.enter_context(nc.Block())

        @block.sync
        def _(sp):
            for credited, n in CREDITS:
                sp.sem_inc(credited, n)
            for c in range(CH):
                sp.dma_start(acc[:, BPC * c:BPC * c + BPC, :], x_blocks[:, BPC * c:BPC * c + BPC, :]).then_inc(x_in[c], 16)
                if c == 1:
                    for dst, src in GATE_CONSTS:
                        sp.dma_start(dst[tuple(slice(None) for _ in dst.shape)], src).then_inc(gate_in, 16)
                    for dst, src in PROJ_CONSTS:
                        sp.dma_start(dst[tuple(slice(None) for _ in dst.shape)], src).then_inc(proj_in, 16)
            for dst, src in CONSTS:
                sp.dma_start(dst[tuple(slice(None) for _ in dst.shape)], src).then_inc(consts_in, 16)
            sp.wait_ge(zero_made, 1)
            sp.dma_start(rows_in[0:TILES // 3 * P, :].rearrange("(n p) d -> p n d", p=P),
                         zero[:, 0:P].unsqueeze(1).broadcast_to([P, TILES // 3, P])).then_inc(rows_zeroed, 16)
            sp.dma_start(rows_in[TILES // 3 * P:2 * TILES // 3 * P, :].rearrange("(n p) d -> p n d", p=P),
                         zero[:, 0:P].unsqueeze(1).broadcast_to([P, TILES // 3, P])).then_inc(rows_zeroed, 16)
            sp.dma_start(rows_in[2 * TILES // 3 * P:, :].rearrange("(n p) d -> p n d", p=P),
                         zero[:, 0:P].unsqueeze(1).broadcast_to([P, TILES // 3, P])).then_inc(rows_zeroed, 16)
            sp.wait_ge(bsplit, 6)
            sp.dma_start(bias_parts, bbp[:, :, :]).then_inc(bias_stored, 16)

            def store_parts(c):
                sp.wait_ge(lo_made, c + 1)
                if not (isinstance(c, int) and c == 0):
                    sp.wait_ge(repd, UNITS * (c - 1) + 1)
                    sp.wait_ge(repu, UNITS * (c - 1) + 1)
                sp.dma_start(part_rows.rearrange("d k w t -> d (k w t)"),
                             parts[:, :, :].rearrange("p k t -> p (k t)")).then_inc(parts_stored, 16)

            def load_stack(c, h):
                sp.wait_ge(parts_stored, 16 * (c + 1))
                for q in range(QUADS):
                    rows = part_rows[32 * q:32 * q + 32].rearrange("(m e) k w t -> (e k) m (w t)", m=4)
                    sp.dma_start(stack[32 * q:32 * q + 3 * EC, h, :, :, :].rearrange("p m w t -> p m (w t)"),
                                 rows).then_inc(stack_in, 16)

            store_parts(0)
            load_stack(0, 0)
            sp.wait_ge(bias_stored, 16)
            sp.wait_ge(scattered, 16 * NB)
            sp.wait_ge(routed, 2)

            weights, biases = {}, {}

            def load_rows(b, i):
                t, s = b * TPB + i, i % 2
                sp.wait_ge(xs_turned, t + (1 if i else 2))
                sp.dma_start(xs[:, s, :], rows_in[bass.ds(t * P, P), :]).then_inc(tile_x_in[s], 16)

            def of_expert(b, i):
                e = sp.value_load(tei[0:1, bass.ds(b * TPB + i, 1)], min_val=0, max_val=E - 1)
                weights[i] = w_exp[bass.ds(e, 1)].rearrange("a p f -> p (a f)")
                biases[i] = bias_parts[bass.ds(e, 1)].rearrange("a k f -> k (a f)")

            def load_w1(b, i):
                t, s = b * TPB + i, i % 2
                of_expert(b, i)
                sp.wait_ge(hidden, t + (1 if i else 2))
                sp.dma_start(wst[:, s, 0:F], weights[i][:, 0:F]).then_inc(tile_w1_in[s], 16)
                sp.dma_start(b1st[:, s, :], biases[i][:, 0:F].rearrange("k (f p) -> k f p", p=P)).then_inc(tile_w1_in[s], 16)

            def load_w2(b, i):
                t, s = b * TPB + i, i % 2
                if i == 0:
                    of_expert(b, i)
                sp.wait_ge(down, t + (1 if i else 2))
                sp.dma_start(wst[:, s, F:], weights[i][:, F:]).then_inc(tile_w2_in[s], 16)
                sp.dma_start(b2st[:, s, :], biases[i][:, F:]).then_inc(tile_w2_in[s], 16)

            def store_rows(b, i):
                t, s = b * TPB + i, i % 2
                sp.wait_ge(ys_copied, t + 1 + 1)
                sp.dma_start(rows_out[bass.ds(t * P, P), :], ysb[:, s, :]).then_inc(ys_stored[s], 16)

            def store_late_rows(b):
                for i in range(TPB):
                    if SLOT_DOWN[i] + 1 >= UB:
                        store_rows(b, i)

            def start(b):
                load_rows(b, 0)
                load_w1(b, 0)
                load_rows(b, 1)

            def batch(b, last):
                for w in range(UB):
                    h, u = divmod(w, UNITS)
                    if not last:
                        for i in range(TPB):
                            if w == SLOT_HIDDEN[i] - 3 and i:
                                load_w1(b, i)
                                if i + 1 < TPB:
                                    load_rows(b, i + 1)
                            if w == min(SLOT_DOWN[i] - 3, UB - 1):
                                load_w2(b, i)
                            if w == SLOT_DOWN[i] + 1:
                                store_rows(b, i)
                    if not (last and h == HALVES - 1):
                        if u == SLOT_STORE:
                            store_parts(b * HALVES + h + 1)
                        if u == SLOT_STACK:
                            load_stack(b * HALVES + h + 1, (h + 1) % 2)

            start(0)
            with sp.Fori(0, B - 2) as b:
                batch(b, False)
                start(b + 1)
                store_late_rows(b)
            batch(B - 2, False)
            store_late_rows(B - 2)
            batch(B - 1, True)
            for c in range(CH):
                sp.wait_ge(combined, BPC * (c + 1))
                if c == CH - 1:
                    sp.wait_ge(acc_added, CH + 2)
                sp.dma_start(out_blocks[:, BPC * c:BPC * c + BPC, :], acc[:, BPC * c:BPC * c + BPC, :]).then_inc(out_stored, 16)
            sp.wait_ge(out_stored, 16 * CH)

        @block.gpsimd
        def _(pool):
            pool.memset(zero[:, :], 0.0).then_inc(zero_made, 1)
            pool.memset(ones[:, :], 1.0).then_inc(const_made, 1)
            pool.memset(onesb[:, :], 1.0).then_inc(const_made, 1)
            pool.wait_ge(bias_ready, 1)
            for c in range(CH):
                pool.wait_ge(xn_made, BPC * (c + 1))
                pool.tensor_tensor(blocks_of(c), blocks_of(c), bias_rep[:, :].unsqueeze(1).broadcast_to([P, BPC, D]),
                                   ALU.add).then_inc(bias_added, 1)
            def bias(n, ins):
                ins.then_inc(bsplit, 1)
                pool.wait_ge(bsplit, n)

            pool.wait_ge(consts_in, 16 * len(CONSTS))
            bias(1, pool.tensor_scalar(bb[:, 0, F:], bb[:, 0, F:], 2.0, None, ALU.mult))
            bias(2, pool.tensor_copy(bbp[:, 0, :], bb[:, 0, :]))
            bias(3, pool.tensor_tensor(bb[:, 1, :], bb[:, 0, :], bbp[:, 0, :], ALU.subtract))
            bias(4, pool.tensor_copy(bbp[:, 1, :], bb[:, 1, :]))
            bias(5, pool.tensor_tensor(bb[:, 2, :], bb[:, 1, :], bbp[:, 1, :], ALU.subtract))
            bias(6, pool.tensor_copy(bbp[:, 2, :], bb[:, 2, :]))
            pool.wait_ge(rms_ready, 1)
            for c in range(CH):
                pool.wait_ge(xt_turned, c + 1)
                pool.tensor_tensor(xr[:, BPC * c:BPC * c + BPC, :], xr[:, BPC * c:BPC * c + BPC, :],
                                   sm[:, 9, BPC * c:BPC * c + BPC].unsqueeze(2).broadcast_to([P, BPC, D]),
                                   ALU.mult).then_inc(xr_made, 1)

            pool.wait_ge(xr_made, CH)
            pool.wait_ge(rows_zeroed, 48)
            pool.wait_ge(routed, 1)
            for j in range(NB):
                pool.indirect_dma_start(out=rows_in[:, :], out_offset=bass.IndirectOffsetOnAxis(ap=posi[:, j:j + 1], axis=0),
                                        in_=xr[:, j, :], in_offset=None).then_inc(scattered, 16)

            def split_rest(c):
                pool.wait_ge(hi_made, c + 1)
                pool.tensor_tensor(rest[:, :], dd_of(c), parts[:, 0, :], ALU.subtract).then_inc(rest_made, 1)

            def split_lo(c):
                pool.wait_ge(mid_made, c + 1)
                pool.tensor_tensor(parts[:, 2, :], rest[:, :], parts[:, 1, :], ALU.subtract).then_inc(lo_made, 1)

            def slot(b, w, first_one, last):
                h, u = divmod(w, UNITS)
                c = b * HALVES + h
                more = not (last and h == HALVES - 1)
                if u == SLOT_REST and more:
                    split_rest(c + 1)
                if u == SLOT_LO and more:
                    split_lo(c + 1)
                if w in (pool_last if last else pool_units):
                    pool.wait_ge(scanned, b * UB + w + 1 + BANKS)
                    pool.wait_ge(crep_ready, c + 1)
                    pool.wait_ge(reduced, 4 * c + u // 4 - 1 + GROUPS)
                    pool.tensor_tensor(ch_[:, u % RING_P, :], hst[:, u, :], crep[:, h, :], ALU.mult).then_inc(pool_p, 1)
                if last:
                    if w == FIRST_GATHER:
                        for s in range(2):
                            pool.wait_ge(ys_stored[s], 16 * (((TPB + 1 - s) // 2) * (B - 1) + 1))
                    for j in gathers(w):
                        if j >= GAT:
                            pool.wait_ge(combined, j - GAT + 1)
                        pool.indirect_dma_start(out=gat[:, j % GAT, :], out_offset=None, in_=rows_out[:, :],
                                                in_offset=bass.IndirectOffsetOnAxis(ap=posi[:, j:j + 1], axis=0)
                                                ).then_inc(gathered[j % GAT], 16)

            batches(pool, slot)

        @block.scalar
        def _(act):
            def turned(c):
                act.wait_ge(xt_turned, c + 1)
                act.activation(dd[:, c, 1, :], bank[c % 2][:, :], ACT.Copy).then_inc(xt_copied, 1)

            def tap(c):
                act.wait_ge(inx_made, c + 1)
                if c >= 2:
                    act.wait_ge(conv_step, 3 * (c - 1))
                    act.wait_ge(pad_made, 1 + c // 2)
                act.activation(xin[c % 2][:, K - 1:], bank[5][:, :], ACT.Identity, bias=col[:, 0:1]).then_inc(xin_copied, 1)
                act.wait_ge(xin_copied, c + 1)
                if c >= 2:
                    act.wait_ge(xc_made, c - 1)
                act.activation(conv[c % 2], xin[c % 2][:, K - 1:], ACT.Identity, bias=col[:, 2:3],
                               scale=cw[:, K - 1:K]).then_inc(tap_made, 1)

            def gate(c):
                act.wait_ge(inres_made, c + 1)
                act.activation(sres[:, c, :], bank[6][:, :], ACT.Silu, bias=col[:, 1:2]).then_inc(sres_made, 1)

            def halves(c):
                tap(c)
                gate(c)

            def convolved(c):
                act.wait_ge(conv_step, 3 * (c + 1))
                act.activation(xc[:, c, :], conv[c % 2], ACT.Silu).then_inc(xc_made, 1)

            def before_softplus(c):
                act.wait_ge(dt_made, c + 1)
                act.activation(dd[:, c, 1, :], bank[c % 2][:, :], ACT.Identity, bias=col[:, 3:4]).then_inc(x_made, 1)

            def exponential(c):
                act.wait_ge(z_made, c + 1)
                act.activation(dd[:, c, 0, :], dd[:, c, 0, :], ACT.Exp).then_inc(e_made, 1)

            def logarithm(c):
                act.wait_ge(e_made, c + 1)
                act.activation(dd[:, c, 0, :], dd[:, c, 0, :], ACT.Ln, bias=1.0).then_inc(l_made, 1)

            def split_hi(c):
                act.wait_ge(du_made, (1 if c == 0 else CH) if isinstance(c, int) else CH)
                if not (isinstance(c, int) and c == 0):
                    act.wait_ge(parts_stored, 16 * c)
                act.activation(parts[:, 0, :], dd_of(c), ACT.Copy).then_inc(hi_made, 1)

            def split_mid(c):
                act.wait_ge(rest_made, c + 1)
                act.activation(parts[:, 1, :], rest[:, :], ACT.Copy).then_inc(mid_made, 1)

            def brep_copy(c, h):
                act.wait_ge(brep_mm, c + 1)
                if not (isinstance(c, int) and c == 0):
                    act.wait_ge(mulb, UNITS * (c - 1) + 1 + BANKS)
                act.activation(brep[:, h, :], bank_f[:, :], ACT.Identity, bias=col[:, 6:7]).then_inc(brep_ready, 1)

            def crep_copy(c, h):
                act.wait_ge(crep_mm, c + 1)
                if not (isinstance(c, int) and c == 0):
                    act.wait_ge(reduced, 4 * (c - 1) + GROUPS)
                act.activation(crep[:, h, :], bank_f[:, :], ACT.Identity, bias=col[:, 7:8]).then_inc(crep_ready, 1)

            turned(0)
            act.wait_ge(bias_mm, 1)
            act.activation(bias_rep[:, :], bank[7][:, 0:D], ACT.Copy).then_inc(bias_ready, 1)
            turned(1)
            halves(0)
            halves(1)
            for c in range(2, CH):
                turned(c)
            convolved(0)
            halves(2)
            convolved(1)
            act.wait_ge(route, 3)
            act.activation(rt[:, 1], rt[:, 0], ACT.Exp).then_inc(rexp_made, 1)
            act.activation(nega[:, 0:1], col[:, 5:6], ACT.Exp).then_inc(expa_made, 1)
            act.wait_ge(consts_in, 16 * len(CONSTS))
            act.activation(sel[:, :], rest[:, 0:P], ACT.Copy).then_inc(sel_made, 1)
            act.activation(blocksel[:, :], rest[0:3 * FC, P:P + F], ACT.Copy).then_inc(sel_made, 1)
            tap(3)
            before_softplus(0)
            exponential(0)
            logarithm(0)
            gate(3)
            convolved(2)
            split_hi(0)
            halves(4)
            convolved(3)
            split_mid(0)
            for c in range(5, CH):
                halves(c)
                if c > 5:
                    before_softplus(c - 5)
                convolved(c - 1)
            before_softplus(CH - 5)
            convolved(CH - 1)
            before_softplus(CH - 4)
            exponential(1)
            exponential(2)
            for c in range(CH - 3, CH):
                before_softplus(c)
                exponential(c - 2)
            exponential(CH - 2)
            exponential(CH - 1)
            for c in range(1, CH):
                logarithm(c)
            brep_copy(0, 0)
            act.wait_ge(bias_stored, 16)
            crep_copy(0, 0)
            act.wait_ge(nega_made, 1)

            def decay(b, w):
                act.wait_ge(repd, b * UB + w + 1)
                act.activation(bank_d[w % 2][:, :], bank_d[w % 2][:, :], ACT.Exp, scale=nega[:, 1:2]).then_inc(exped, 1)

            decay(0, 0)
            decay(0, 1)

            def gain(b, i):
                act.wait_ge(xs_turned, b * TPB + i + 1 + SLOTS)
                act.activation(xsT[:, :], bank_m[:, 0:P], ACT.Copy, scale=rms).then_inc(xs_copied, 1)

            def half_tanh(b, i):
                t = b * TPB + i
                act.wait_ge(hidden, t + 1 + SLOTS)
                act.wait_ge(gated, t + 1)
                act.activation(th[:, :], bank_h[:, :], ACT.Tanh, scale=0.5).then_inc(tanh_made, 1)

            def copy_rows(b, i):
                t, s = b * TPB + i, i % 2
                act.wait_ge(down, t + 1 + SLOTS)
                act.wait_ge(ys_stored[s], 16 * (b * ((TPB + 1 - s) // 2) + i // 2 + 1))
                act.activation(ysb[:, s, :], bank_m[:, P:2 * P], ACT.Copy).then_inc(ys_copied, 1)

            def slot(b, w, first_one, last):
                h, u = divmod(w, UNITS)
                c = b * HALVES + h
                more = not (last and h == HALVES - 1)
                hn = (h + 1) % 2
                if w + AHEAD < UB:
                    decay(b, w + AHEAD)
                elif not last:
                    decay(b + 1, w + AHEAD - UB)
                turns = tiles_at(SLOT_TURN, b, w, first_one, last)
                for tile in turns[:1] if w == HEAD else []:
                    gain(*tile)
                for tile in tiles_at(SLOT_HIDDEN, b, w, first_one, last):
                    half_tanh(*tile)
                for tile in turns[1:] if w == HEAD else turns:
                    gain(*tile)
                for tile in tiles_at(SLOT_DOWN, b, w, first_one, last):
                    copy_rows(*tile)
                if more and u == SLOT_HI:
                    split_hi(c + 1)
                if more and u == SLOT_MID:
                    split_mid(c + 1)
                if more and u == SLOT_B[h]:
                    brep_copy(c + 1, hn)
                if more and u == SLOT_C[h]:
                    crep_copy(c + 1, hn)

            batches(act, slot)

        @block.vector
        def _(dve):
            steps = [0]

            def stat(ins):
                steps[0] += 1
                ins.then_inc(small, 1)
                dve.wait_ge(small, steps[0])

            dve.memset(xin[0][:, 0:K - 1], 0.0).then_inc(pad_made, 1)

            def inverse_root(value, result, tmp):
                stat(dve.tensor_scalar(result.bitcast(I32), value.bitcast(I32), 1, None, ALU.logical_shift_right))
                stat(dve.tensor_scalar(result.bitcast(I32), result.bitcast(I32), -1.0, ROOT_MAGIC, ALU.mult, ALU.add))
                for _ in range(3):
                    stat(dve.tensor_tensor(tmp, result, result, ALU.mult))
                    stat(dve.scalar_tensor_tensor(out=tmp, in0=tmp, scalar=-0.5, in1=value, op0=ALU.mult, op1=ALU.mult))
                    stat(dve.scalar_tensor_tensor(out=result, in0=tmp, scalar=1.5, in1=result, op0=ALU.add, op1=ALU.mult))

            def statistics(lo, hi):
                blocks = slice(BPC * lo, BPC * hi)
                for j in range(BPC * lo, BPC * hi):
                    if j % BPC == 0:
                        dve.wait_ge(x_in[j // BPC], 16)
                    dve.bn_stats(stats[:, j, :], acc[:, j, :]).then_inc(stat_made, 1)
                dve.wait_ge(stat_made, BPC * hi)
                for j in range(BPC * lo, BPC * hi):
                    dve.bn_aggr(mv[:, j, :], stats[:, j, :]).then_inc(aggregated, 1)
                dve.wait_ge(aggregated, BPC * hi)
                stat(dve.tensor_scalar(sm[:, 0, blocks], mv[:, blocks, 1], LN_EPS, None, ALU.add))
                inverse_root(sm[:, 0, blocks], sm[:, 4, blocks], sm[:, 3, blocks])

            def normalise(c):
                for j in range(BPC):
                    n = BPC * c + j
                    dve.tensor_scalar(xn[:, n, :], acc[:, n, :], mv[:, n, 0:1], sm[:, 4, n:n + 1],
                                      ALU.subtract, ALU.mult).then_inc(xn_made, 1)

            def convolve(c):
                if c % 2:
                    dve.wait_ge(xin_copied, c)
                    dve.tensor_copy(xin[1][:, 0:K - 1], xin[0][:, L:L + K - 1]).then_inc(pad_made, 1)
                    dve.wait_ge(pad_made, 2 + c // 2)
                dve.wait_ge(tap_made, c + 1)
                for n, k in enumerate(range(K - 2, -1, -1)):
                    if n:
                        dve.wait_ge(conv_step, 3 * c + n)
                    dve.scalar_tensor_tensor(out=conv[c % 2], in0=xin[c % 2][:, k:k + L], scalar=cw[:, k:k + 1],
                                             in1=conv[c % 2], op0=ALU.mult, op1=ALU.add).then_inc(conv_step, 1)

            def add_skip_projection(c):
                dve.wait_ge(skip_made, c + 1)
                dve.wait_ge(bias_added, c + 1)
                for i, n in enumerate(skip_banks(c)):
                    o = BPC * c + 2 * i
                    both = bank[n][:, 0:2 * (D + E)].rearrange("p (j d) -> p j d", d=D + E)
                    dve.tensor_copy(logits[:, o:o + 2, :], both[:, :, D:]).then_inc(gate_made, 1)
                    dve.tensor_tensor(acc[:, o:o + 2, :], acc[:, o:o + 2, :], both[:, :, 0:D], ALU.add).then_inc(skip_added, 1)

            def low_copy(c):
                dve.wait_ge(low_made, c + 1)
                if c >= 2:
                    dve.wait_ge(dt_made, c - 1)
                dve.tensor_scalar(low[c % 2], bank[2 + c % 2][0:R, :], lowb, None, ALU.add).then_inc(low_copied, 1)

            def cut(c):
                dve.wait_ge(x_made, c + 1)
                dve.tensor_scalar(dd[:, c, 0, :], dd[:, c, 1, :], SOFTPLUS_CUT, None, ALU.min).then_inc(z_made, 1)

            def delta(c):
                dve.wait_ge(l_made, c + 1)
                dve.tensor_tensor(dd[:, c, 0, :], dd[:, c, 0, :], dd[:, c, 1, :], ALU.max).then_inc(delta_made, 1)

            def delta_u(c):
                dve.wait_ge(delta_made, c + 1)
                dve.tensor_tensor(dd[:, c, 1, :], dd[:, c, 0, :], xc[:, c, :], ALU.mult).then_inc(du_made, 1)

            statistics(0, 2)
            normalise(0)
            normalise(1)
            dve.wait_ge(gate_in, 16 * len(GATE_CONSTS))
            dve.tensor_scalar(wsg[:, D:], wsg[:, D:], rms, None, ALU.mult).then_inc(gatew_made, 1)
            statistics(2, CH)
            for c in range(2, CH):
                normalise(c)
                if c >= 3:
                    add_skip_projection(c - 3)
            stat(dve.tensor_tensor(sm[:, 8, :], mv[:, :, 1], sm[:, 4, :], ALU.mult))
            stat(dve.tensor_tensor(sm[:, 8, :], sm[:, 8, :], sm[:, 4, :], ALU.mult))
            stat(dve.tensor_scalar(sm[:, 5, :], sm[:, 8, :], RMS_EPS, None, ALU.add))
            inverse_root(sm[:, 5, :], sm[:, 9, :], sm[:, 3, :])
            dve.tensor_copy(sm[:, 7, 0:1], sm[:, 9, 0:1]).then_inc(rms_ready, 1)
            convolve(0)
            add_skip_projection(CH - 3)
            convolve(1)
            add_skip_projection(CH - 2)
            add_skip_projection(CH - 1)

            done = [0]

            def step(ins):
                done[0] += 1
                ins.then_inc(route, 1)
                dve.wait_ge(route, done[0])

            def per_token(v):
                return v.unsqueeze(1).broadcast_to([P, E, NB])

            def by_token(v):
                return v.rearrange("p e j -> p j e")

            dve.wait_ge(gate_made, 2 * CH)
            dve.wait_ge(consts_in, 16 * len(CONSTS))
            dve.wait_ge(const_made, 2)
            step(dve.tensor_tensor(rt[:, 0], logits[:, :, :].rearrange("p j e -> p e j"), per_token(sm[:, 9, :]), ALU.mult))
            step(dve.tensor_reduce(sm[:, 10, :], by_token(rt[:, 0]), AX_X, ALU.max))
            step(dve.tensor_tensor(rt[:, 0], rt[:, 0], per_token(sm[:, 10, :]), ALU.subtract))
            low_copy(0)
            convolve(2)
            cut(0)
            dve.wait_ge(rexp_made, 1)
            step(dve.tensor_reduce(sm[:, 11, :], by_token(rt[:, 1]), AX_X, ALU.add))
            step(dve.reciprocal(score[:, :], sm[:, 11, :]))
            step(dve.tensor_scalar(score[:, :], score[:, :], 0.5, None, ALU.mult))
            step(dve.scalar_tensor_tensor(out=rt[:, 2], in0=rt[:, 0], scalar=0.0, in1=first[:, :, :],
                                          op0=ALU.is_equal, op1=ALU.mult))
            step(dve.tensor_reduce(sm[:, 10, :], by_token(rt[:, 2]), AX_X, ALU.max))
            step(dve.tensor_tensor(rt[:, 3], rt[:, 2], per_token(sm[:, 10, :]), ALU.is_equal))
            one_hot = done[0]
            assert one_hot == 9
            delta(0)
            delta_u(0)
            convolve(3)
            low_copy(1)
            dve.wait_ge(sel_made, 2)
            dve.wait_ge(hi_made, 1)
            dve.tensor_tensor(rest[:, :], dd_of(0), parts[:, 0, :], ALU.subtract).then_inc(rest_made, 1)
            dve.wait_ge(expa_made, 1)
            dve.tensor_scalar(nega[:, 1:2], nega[:, 0:1], -1.0, None, ALU.mult).then_inc(nega_made, 1)
            dve.wait_ge(rank_made, 1)
            within = bank[7][:, 0:E * NB].rearrange("p (e j) -> p e j", e=E)
            total = bank[7][:, E * NB:2 * E * NB].rearrange("p (e j) -> p e j", e=E)
            for e in range(E):
                step(dve.tensor_tensor_scan(rt[:, 4, e, :], ones[:, 0:NB], total[:, e, :], 0.0, ALU.mult, ALU.add))
            step(dve.tensor_scalar(cnti[:, :], rt[:, 4, :, NB - 1], float(P - 1), None, ALU.add))
            step(dve.tensor_scalar(cnti[:, :], cnti[:, :], 7, 7, ALU.logical_shift_right, ALU.logical_shift_left))
            step(dve.tensor_copy(cnt[:, 1, :], cnti[:, :]))
            step(dve.tensor_tensor_scan(cnt[:, 2, :], ones[:, 0:E], cnt[:, 1, :], 0.0, ALU.mult, ALU.add))
            step(dve.tensor_tensor(cnt[:, 3, :], cnt[:, 2, :], cnt[:, 1, :], ALU.subtract))
            step(dve.tensor_tensor(rt[:, 5], within, rt[:, 4], ALU.add))
            step(dve.tensor_tensor(rt[:, 5], rt[:, 5], total, ALU.subtract))
            step(dve.tensor_tensor(rt[:, 5], rt[:, 5], cnt[:, 3, :].unsqueeze(2).broadcast_to([P, E, NB]), ALU.add))
            step(dve.tensor_tensor(rt[:, 5], rt[:, 5], rt[:, 3], ALU.mult))
            step(dve.tensor_reduce(sm[:, 10, :], by_token(rt[:, 5]), AX_X, ALU.add))
            dve.tensor_copy(posi[:, :], sm[:, 10, :]).then_inc(routed, 1)
            step(dve.tensor_tensor(tcmp[:, :, :], tilec[:, :, :], cnt[0:1, 2, :].unsqueeze(1).broadcast_to([1, TILES, E]), ALU.is_ge))
            step(dve.tensor_reduce(tef[:, :], tcmp[:, :, :], AX_X, ALU.add))
            dve.tensor_scalar(tei[:, :], tef[:, :], float(E - 1), None, ALU.min).then_inc(routed, 1)

            dve.wait_ge(mid_made, 1)
            dve.tensor_tensor(parts[:, 2, :], rest[:, :], parts[:, 1, :], ALU.subtract).then_inc(lo_made, 1)

            for c in range(4, CH):
                convolve(c)
                low_copy(c - 2)
                if c > 4:
                    cut(c - 4)
            for c in range(CH - 2, CH):
                low_copy(c)
                cut(c - 2)
            cut(CH - 2)
            cut(CH - 1)
            for c in range(1, CH):
                delta(c)
                if c > 1:
                    delta_u(c - 1)
            delta_u(CH - 1)

            def drive(b, w):
                h, u = divmod(w, UNITS)
                dve.wait_ge(repu, b * UB + w + 1)
                dve.wait_ge(brep_ready, b * HALVES + h + 1)
                dve.tensor_tensor(dbu[:, w % RING_B, :], bank_u[w % 2][:, :], brep[:, h, :], ALU.mult).then_inc(mulb, 1)

            def scan(b, w, last):
                h, u = divmod(w, UNITS)
                dve.wait_ge(exped, b * UB + w + 1)
                dve.wait_ge(mulb, b * UB + w + 1 + BANKS)
                v, units_p, units_d = (w - UNITS, pool_last, DVE_P_LAST) if last and w >= UNITS else (w - UNITS, pool_units, DVE_P)
                back = 0 if v >= 0 else 1
                v %= UB
                if v in units_d:
                    dve.wait_ge(dve_p, (b - back) * ND + before(units_d, v) + 1 + ND)
                else:
                    dve.wait_ge(pool_p, (b - back) * NP + before(units_p, v) + 1 + NP)
                if w == UNITS // 2:
                    dve.wait_ge(scattered, 16 * NB)
                start = hst[:, u, L - 1:L] if h else 0.0
                dve.tensor_tensor_scan(hst[:, u, :], bank_d[w % 2][:, :], dbu[:, w % RING_B, :], start,
                                       ALU.mult, ALU.add).then_inc(scanned, 1)

            drive(0, 0)
            drive(0, 1)

            def combine(j):
                dve.wait_ge(gathered[j % GAT], 16 * (j // GAT + 1))
                dve.scalar_tensor_tensor(out=acc[:, j, :], in0=gat[:, j % GAT, :], scalar=score[:, j:j + 1],
                                         in1=acc[:, j, :], op0=ALU.mult, op1=ALU.add).then_inc(combined, 1)

            def add_skip(c):
                dve.wait_ge(reduced, 4 * (c + 1) + GROUPS)
                dve.scalar_tensor_tensor(out=y1[:, :], in0=row_of(xc, c), scalar=col[:, 4:5], in1=bank_y[:, :],
                                         op0=ALU.mult, op1=ALU.add).then_inc(y1_made, 1)

            def gate_sum(c):
                dve.wait_ge(y1_made, c + 1 + 1)
                dve.wait_ge(proj_made, c)
                dve.tensor_tensor(yg[:, :], y1[:, :], row_of(sres, c), ALU.mult).then_inc(yg_made, 1)

            def add_projection(c):
                dve.wait_ge(proj_made, c + 1)
                dve.tensor_tensor(blocks_of(c), blocks_of(c), bank_f[:, :].rearrange("p (j d) -> p j d", d=D),
                                  ALU.add).then_inc(acc_added, 1)

            def slot(b, w, first_one, last):
                h, u = divmod(w, UNITS)
                c = b * HALVES + h
                scan(b, w, last)
                ends = u < HEAD and not (first_one and h == 0)
                if ends and u == 2:
                    gate_sum(c - 1)
                for bt, i in tiles_at(SLOT_GATE, b, w, first_one, last):
                    t = bt * TPB + i
                    dve.wait_ge(tanh_made, t + 1)
                    dve.wait_ge(down, t + (1 if i else 2))
                    dve.scalar_tensor_tensor(out=hid[:, i % 2, :], in0=th[:, :], scalar=1.0, in1=bank_h[:, :],
                                             op0=ALU.add, op1=ALU.mult).then_inc(gated, 1)
                if w + AHEAD < UB:
                    drive(b, w + AHEAD)
                elif not last:
                    drive(b + 1, w + AHEAD - UB)
                if last:
                    for j in combines(w):
                        combine(j)
                if w in (DVE_P_LAST if last else DVE_P):
                    dve.wait_ge(scanned, b * UB + w + 1 + BANKS)
                    dve.wait_ge(crep_ready, c + 1)
                    dve.wait_ge(reduced, 4 * c + u // 4 - 1 + GROUPS)
                    dve.tensor_tensor(ch_[:, u % RING_P, :], hst[:, u, :], crep[:, h, :], ALU.mult).then_inc(dve_p, 1)
                if ends and u == 1:
                    add_skip(c - 1)
                if ends and u == 3:
                    add_projection(c - 1)

            batches(dve, slot)
            for w in range(UB, UB + GATHER_LAG + 1):
                for j in combines(w):
                    combine(j)
            add_skip(CH - 1)
            gate_sum(CH - 1)
            dve.wait_ge(combined, NB)
            add_projection(CH - 1)

        @block.tensor
        def _(pe):
            def turn(c):
                pe.wait_ge(xn_made, BPC * (c + 1))
                if c >= 2:
                    pe.wait_ge(xt_copied, c - 1)
                for j in range(BPC):
                    mm = pe.transpose(bank[c % 2][:, P * j:P * j + P], xn[:, BPC * c + j, :], ident[:, :])
                mm.then_inc(xt_turned, 1)

            def halves(c):
                xt = dd[:, c, 1, :]
                pe.wait_ge(xt_copied, c + 1)
                if c >= 1:
                    pe.wait_ge(xin_copied, c)
                pe.matmul(bank[5][:, :], win[:, 0:D], xt, start=True, stop=True).then_inc(inx_made, 1)
                if c >= 1:
                    pe.wait_ge(sres_made, c)
                pe.matmul(bank[6][:, :], win[:, D:2 * D], xt, start=True, stop=True).then_inc(inres_made, 1)

            def skip_and_gate(c):
                pe.wait_ge(xt_copied, c + 1)
                if c >= 2:
                    pe.wait_ge(skip_added, 2 * (c - 1))
                for j in range(BPC):
                    o = (D + E) * (j % 2)
                    mm = pe.matmul(bank[skip_banks(c)[j // 2]][:, o:o + D + E], dd[:, c, 1, P * j:P * j + P], wsg[:, :],
                                   start=True, stop=True)
                mm.then_inc(skip_made, 1)

            def low_rank(c):
                pe.wait_ge(xc_made, c + 1)
                if c == 0:
                    pe.wait_ge(skip_added, 2 * CH)
                if c >= 2:
                    pe.wait_ge(low_copied, c - 1)
                pe.matmul(bank[2 + c % 2][0:R, :], wx[:, 0:R], xc[:, c, :], start=True, stop=True).then_inc(low_made, 1)

            def delta_of_low(c):
                pe.wait_ge(low_copied, c + 1)
                if c >= 2:
                    pe.wait_ge(x_made, c - 1)
                pe.matmul(bank[c % 2][:, :], wdt[:, :], low[c % 2], start=True, stop=True).then_inc(dt_made, 1)

            def brep_matmul(c, h):
                if isinstance(c, int) and c == 0:
                    pe.wait_ge(routed, 1)
                else:
                    pe.wait_ge(crep_ready, c)
                    pe.wait_ge(acc_added, c + (SLOT_B[h] >= SLOT_PROJECT))
                pe.matmul(bank_f[:, :], wx[:, R:R + P], row_of(xc, c), start=True, stop=True).then_inc(brep_mm, 1)

            def crep_matmul(c, h):
                pe.wait_ge(brep_ready, c + 1)
                if SLOT_B[h] < SLOT_PROJECT <= SLOT_C[h] and not (isinstance(c, int) and c == 0):
                    pe.wait_ge(acc_added, c + 1)
                pe.matmul(bank_f[:, :], wx[:, R + P:R + 2 * P], row_of(xc, c), start=True, stop=True).then_inc(crep_mm, 1)

            pe.wait_ge(gate_in, 16 * len(GATE_CONSTS))
            turn(0)
            pe.wait_ge(proj_in, 16 * len(PROJ_CONSTS))
            pe.wait_ge(const_made, 2)
            pe.matmul(bank[7][:, 0:D], ones[0:2, :], ob[:, :], start=True, stop=True).then_inc(bias_mm, 1)
            halves(0)
            turn(1)
            halves(1)
            pe.wait_ge(gatew_made, 1)
            skip_and_gate(0)
            pe.wait_ge(bias_ready, 1)
            skip_and_gate(1)
            for c in range(2, CH):
                turn(c)
                if c >= 3:
                    skip_and_gate(c - 1)
            skip_and_gate(CH - 1)
            halves(2)
            pe.wait_ge(consts_in, 16 * len(CONSTS))
            low_rank(0)
            halves(3)
            delta_of_low(0)
            halves(4)
            low_rank(1)
            pe.wait_ge(route, 9)
            one_hot = rt[:, 3].rearrange("p e j -> p (e j)")
            pe.matmul(bank[7][:, 0:E * NB], strict[:, :], one_hot, start=True, stop=True)
            pe.matmul(bank[7][:, E * NB:2 * E * NB], ones[:, :], one_hot, start=True, stop=True).then_inc(rank_made, 1)
            halves(5)
            low_rank(2)
            halves(6)
            delta_of_low(1)
            low_rank(3)
            halves(7)
            delta_of_low(2)
            low_rank(4)
            for c in range(CH - 3, CH):
                delta_of_low(c - 2)
                low_rank(c)
            delta_of_low(CH - 2)
            delta_of_low(CH - 1)
            brep_matmul(0, 0)
            crep_matmul(0, 0)

            def rep_u(b, w):
                h, u = divmod(w, UNITS)
                m, q = divmod(u, QUADS)
                if u == 0:
                    pe.wait_ge(stack_in, 16 * QUADS * (b * HALVES + h + 1))
                pe.wait_ge(mulb, b * UB + w - 1 + BANKS)
                rows = slice(32 * q, 32 * q + 3 * EC)
                pe.matmul(bank_u[w % 2][:, :], sel[rows, :], stack[rows, h, m, 1, :], start=True, stop=True,
                          tile_position=(32 * q, 0)).then_inc(repu, 1)

            def rep_d(b, w):
                h, u = divmod(w, UNITS)
                m, q = divmod(u, QUADS)
                pe.wait_ge(scanned, b * UB + w - 1 + BANKS)
                rows = slice(32 * q, 32 * q + 3 * EC)
                pe.matmul(bank_d[w % 2][:, :], sel[rows, :], stack[rows, h, m, 0, :], start=True, stop=True,
                          tile_position=(32 * q, 0)).then_inc(repd, 1)

            pe.wait_ge(low_copied, CH)
            pe.wait_ge(x_made, CH)
            pe.wait_ge(sel_made, 2)
            for w in range(AHEAD):
                rep_u(0, w)
                rep_d(0, w)
            rep_u(0, AHEAD)

            def reduce(b, h, m, last):
                c = b * HALVES + h
                end = h * UNITS + 4 * m + 4
                units_p, units_d = (pool_last, DVE_P_LAST) if last else (pool_units, DVE_P)
                pe.wait_ge(pool_p, b * NP + before(units_p, end) + NP)
                pe.wait_ge(dve_p, b * ND + before(units_d, end) + ND)
                if m == 0:
                    pe.wait_ge(y1_made, c + 1)
                for q in range(QUADS):
                    mm = pe.matmul(bank_y[32 * q:32 * q + 32, :], red[:, m, :], ch_[:, (4 * m + q) % RING_P, :],
                                   start=(m == 0), stop=(m == 3), tile_position=(0, 32 * q))
                mm.then_inc(reduced, 1)

            def project(c, with_b, with_c):
                pe.wait_ge(yg_made, c + 1)
                pe.wait_ge(brep_ready, with_b)
                pe.wait_ge(crep_ready, with_c)
                for j in range(BPC):
                    mm = pe.matmul(bank_f[:, P * j:P * j + P], yg[:, P * j:P * j + P], wout[:, :], start=True, stop=True)
                mm.then_inc(proj_made, 1)

            def turn_rows(b, i):
                t, s = b * TPB + i, i % 2
                pe.wait_ge(tile_x_in[s], 16 * (b * ((TPB + 1 - s) // 2) + i // 2 + 1))
                pe.wait_ge(ys_copied, t + 1 - min(i, 2))
                pe.transpose(bank_m[:, 0:P], xs[:, s, :], ident[:, :]).then_inc(xs_turned, 1)

            def make_hidden(b, i):
                t, s = b * TPB + i, i % 2
                pe.wait_ge(tile_w1_in[s], 32 * (b * ((TPB + 1 - s) // 2) + i // 2 + 1))
                pe.wait_ge(xs_copied, t + 1)
                pe.wait_ge(gated, t + 1)
                pe.matmul(bank_h[:, :], b1st[:, s, :], blocksel[:, :], start=True, stop=False)
                for f in range(FC):
                    mm = pe.matmul(bank_h[:, P * f:P * f + P], wst[:, s, P * f:P * f + P], xsT[:, :],
                                   start=False, stop=(f == FC - 1))
                mm.then_inc(hidden, 1)

            def make_down(b, i):
                t, s = b * TPB + i, i % 2
                pe.wait_ge(tile_w2_in[s], 32 * (b * ((TPB + 1 - s) // 2) + i // 2 + 1))
                pe.wait_ge(ys_copied, t + 1)
                pe.wait_ge(xs_copied, t + 1 + min(2, TPB - 1 - i))
                pe.wait_ge(gated, t + 1 + 1)
                pe.matmul(bank_m[:, P:2 * P], onesb[:, :], b2st[:, s, :], start=True, stop=False)
                for f in range(FC):
                    mm = pe.matmul(bank_m[:, P:2 * P], hid[:, s, P * f:P * f + P],
                                   wst[:, s, F + D * f:F + D * f + D], start=False, stop=(f == FC - 1))
                mm.then_inc(down, 1)

            def slot(b, w, first_one, last):
                h, u = divmod(w, UNITS)
                c = b * HALVES + h
                more = not (last and h == HALVES - 1)
                ends = u < HEAD and not (first_one and h == 0)
                for ahead, rep in ((AHEAD, rep_d), (AHEAD + 1, rep_u)):
                    if w + ahead < UB:
                        rep(b, w + ahead)
                    elif not last:
                        rep(b + 1, w + ahead - UB)
                if u in SLOTS_SUM:
                    reduce(b, h, SLOTS_SUM.index(u), last)
                if ends and u == SLOT_SUM_LAST:
                    if h:
                        reduce(b, h - 1, 3, last)
                    else:
                        reduce(b - 1, HALVES - 1, 3, last)
                if more and u == SLOT_B[h]:
                    brep_matmul(c + 1, h)
                if more and u == SLOT_C[h]:
                    crep_matmul(c + 1, h)
                if ends and u == SLOT_PROJECT:
                    project(c - 1, c + 1 + (more and SLOT_B[h] < SLOT_PROJECT), c + 1 + (more and SLOT_C[h] < SLOT_PROJECT))
                turns = tiles_at(SLOT_TURN, b, w, first_one, last)
                for tile in turns[:1] if w == HEAD else []:
                    turn_rows(*tile)
                for tile in tiles_at(SLOT_HIDDEN, b, w, first_one, last):
                    make_hidden(*tile)
                for tile in tiles_at(SLOT_DOWN, b, w, first_one, last):
                    make_down(*tile)
                for tile in turns[1:] if w == HEAD else turns:
                    turn_rows(*tile)

            batches(pe, slot)
            reduce(B - 1, HALVES - 1, 3, True)
            project(CH - 1, CH, CH)


def kernel(**inputs):
    import numpy as np
    import concourse.bacc as bacc
    from concourse.bass_utils import run_bass_kernel_spmd as run

    a = {k: np.asarray(v) for k, v in inputs.items()}
    at = lambda n: a["L0_attn_" + n]
    ff = lambda n: a["L0_ffn_" + n]
    xp = at("x_proj_w").T
    xb = at("x_proj_b")
    cols = np.stack([at("in_proj_b")[:D], at("in_proj_b")[D:], at("conv_b"), at("dt_proj_b"), at("D_param"),
                     np.repeat(at("A_log")[0], EC), np.repeat(xb[R:R + N], EC), np.repeat(xb[R + N:], EC),
                     np.concatenate([xb[:R], xb[:R]]), ff("rms_w")] + [at("conv_w")[:, 0, k] for k in range(K)], axis=1)
    w1 = ff("W1")
    w2 = ff("W2").reshape(E, FC, P, D).transpose(0, 2, 1, 3).reshape(E, P, FC * D)
    n = np.arange(P)
    sel = np.zeros((P, P), np.float32)
    for q in range(QUADS):
        for e in range(EC):
            for k in range(3):
                sel[32 * q + 3 * e + k, e::EC] = 1.0
    red = np.zeros((P, 4, 32), np.float32)
    for m in range(4):
        red[n, m, EC * m + n % EC] = 1.0
    arrays = {
        "x": at("x"), "w_in": at("in_proj_w").T,
        "w_x": np.concatenate([xp[:, :R], np.repeat(xp[:, R:R + N], EC, axis=1), np.repeat(xp[:, R + N:], EC, axis=1)], axis=1),
        "w_dt": at("dt_proj_w").T, "w_out": at("out_proj_w").T, "w_skip": at("skip_proj_w").T, "w_gate": ff("gate_w").T,
        "w_exp": np.concatenate([w1, w2], axis=2), "b1b2": np.concatenate([ff("b1"), ff("b2")], axis=1),
        "cols": cols,
        "out_b2": np.stack([at("out_proj_b"), at("skip_proj_b")]),
        "ident": np.eye(P, dtype=np.float32), "strict": np.triu(np.ones((P, P), np.float32), 1), "sel": sel,
        "blocksel": np.tile(np.repeat(np.eye(FC, dtype=np.float32), P, axis=1), (3, 1)), "red": red,
        "first": np.ascontiguousarray(np.broadcast_to((E - np.arange(E, dtype=np.float32))[None, :, None], (P, E, NB))),
        "tiles": np.ascontiguousarray(np.broadcast_to((P * np.arange(TILES, dtype=np.float32))[None, :, None], (1, TILES, E))),
    }
    nc = bacc.Bacc("TRN2", target_bir_lowering=False, num_devices=1)
    arrays = {f"in_{k}_dram": np.ascontiguousarray(v) for k, v in arrays.items()}
    args = [nc.dram_tensor(k, v.shape, mybir.dt.from_np(v.dtype), kind="ExternalInput").ap() for k, v in arrays.items()]
    args.append(nc.dram_tensor("out_0_dram", (B, T, D), F32, kind="ExternalOutput").ap())
    block_program(nc, *args)
    r = run(nc, [arrays], core_ids=[0])
    return r.results[0]["out_0_dram"]
```
